# Optimizing a Trainium2 kernel written in Bass

```python
import numpy as np
import jax
import jax.numpy as jnp

def _softmax(x, axis=-1):
    return jax.nn.softmax(x, axis=axis)

def _gelu(x):
    return jax.nn.gelu(x, approximate=True)

def _silu(x):
    return jax.nn.silu(x)

def _sigmoid(x):
    return jax.nn.sigmoid(x)

def _layernorm(x, axis=-1, eps=1e-05):
    m = jnp.mean(x, axis=axis, keepdims=True)
    v = jnp.var(x, axis=axis, keepdims=True)
    return (x - m) / jnp.sqrt(v + eps)

def _scatter_add(tgt, idx, src, axis=0):
    return tgt.at[idx].add(src)

def _segment_sum(src, seg, n):
    return jax.ops.segment_sum(src, seg, n)
kernel_name = 'mk_macaron_d1_jaxref_r8_71a774'

def setup_inputs(seed: int=0):
    np.random.seed(seed)
    _w = jnp.asarray

    def _L0_attn_setup():
        import jax, jax.numpy as jnp
        import numpy as np
        from jax import lax
        BLOCKS = 16
        NUM_HEADS = 8
        KEY_DIM = 64
        WIDTH = 64
        D_MODEL = 256

        def _forward(x, conv_w, conv_b, wq, bq, wk, bk, wv, bv, wo, bo, proj_w, proj_b):
            N, T, D = x.shape
            xp = jnp.pad(x, ((0, 0), (2, 0), (0, 0)))
            qkv = lax.conv_general_dilated(xp, conv_w, window_strides=(1,), padding='VALID', dimension_numbers=('NWC', 'WIO', 'NWC')) + conv_b
            q, k, v = jnp.split(qkv, 3, axis=-1)
            block_len = T // BLOCKS
            qb = q.reshape(N * BLOCKS, block_len, WIDTH)
            kb = k.reshape(N * BLOCKS, block_len, WIDTH)
            vb = v.reshape(N * BLOCKS, block_len, WIDTH)
            qh = jnp.einsum('bsd,dhk->bshk', qb, wq) + bq
            kh = jnp.einsum('bsd,dhk->bshk', kb, wk) + bk
            vh = jnp.einsum('bsd,dhk->bshk', vb, wv) + bv
            scale = 1.0 / jnp.sqrt(jnp.asarray(KEY_DIM, qh.dtype))
            scores = jnp.einsum('bqhk,bshk->bhqs', qh * scale, kh)
            causal = jnp.tril(jnp.ones((block_len, block_len), bool))
            scores = jnp.where(causal[None, None], scores, jnp.asarray(-1000000000.0, scores.dtype))
            attn = jax.nn.softmax(scores, axis=-1)
            ctx = jnp.einsum('bhqs,bshk->bqhk', attn, vh)
            mha_out = jnp.einsum('bqhk,hko->bqo', ctx, wo) + bo
            mha_out = mha_out.reshape(N, T, WIDTH)
            out = mha_out @ proj_w + proj_b
            return out
        key = jax.random.key(seed)
        ks = jax.random.split(key, 8)
        N, T = (4, 512)
        s = lambda *sh: 0.02
        x = jax.random.normal(ks[0], (N, T, D_MODEL), jnp.float32)
        conv_w = jax.random.normal(ks[1], (3, D_MODEL, 3 * WIDTH), jnp.float32) * 0.02
        conv_b = jnp.zeros((3 * WIDTH,), jnp.float32)
        wq = jax.random.normal(ks[2], (WIDTH, NUM_HEADS, KEY_DIM), jnp.float32) * 0.05
        wk = jax.random.normal(ks[3], (WIDTH, NUM_HEADS, KEY_DIM), jnp.float32) * 0.05
        wv = jax.random.normal(ks[4], (WIDTH, NUM_HEADS, KEY_DIM), jnp.float32) * 0.05
        bq = jnp.zeros((NUM_HEADS, KEY_DIM), jnp.float32)
        bk = jnp.zeros((NUM_HEADS, KEY_DIM), jnp.float32)
        bv = jnp.zeros((NUM_HEADS, KEY_DIM), jnp.float32)
        wo = jax.random.normal(ks[5], (NUM_HEADS, KEY_DIM, WIDTH), jnp.float32) * 0.05
        bo = jnp.zeros((WIDTH,), jnp.float32)
        proj_w = jax.random.normal(ks[6], (WIDTH, D_MODEL), jnp.float32) * 0.05
        proj_b = jnp.zeros((D_MODEL,), jnp.float32)
        return dict(x=x, conv_w=conv_w, conv_b=conv_b, wq=wq, bq=bq, wk=wk, bk=bk, wv=wv, bv=bv, wo=wo, bo=bo, proj_w=proj_w, proj_b=proj_b)
    _L0_attn_in = _L0_attn_setup()

    def _L0_ffn_setup():
        import jax, jax.numpy as jnp
        import numpy as np
        from jax import lax
        TOP_K = 2
        NORM_TOPK = True
        W_SCALE = 0.02
        key = jax.random.key(seed)
        k1, k2, k3, k4 = jax.random.split(key, 4)
        B, S, D = (4, 256, 256)
        E, H = (8, 176)
        x = jax.random.normal(k1, (B, S, D), dtype=jnp.float32)
        gate_up_proj = jax.random.normal(k2, (E, 2 * H, D), dtype=jnp.float32) * W_SCALE
        down_proj = jax.random.normal(k3, (E, D, H), dtype=jnp.float32) * W_SCALE
        router_w = jax.random.normal(k4, (E, D), dtype=jnp.float32) * W_SCALE
        return {'x': x, 'gate_up_proj': gate_up_proj, 'down_proj': down_proj, 'router_w': router_w}
    _L0_ffn_in = _L0_ffn_setup()
    _d = {'L0_attn_x': _L0_attn_in['x'], 'L0_attn_conv_w': _L0_attn_in['conv_w'], 'L0_attn_conv_b': _L0_attn_in['conv_b'], 'L0_attn_wq': _L0_attn_in['wq'], 'L0_attn_bq': _L0_attn_in['bq'], 'L0_attn_wk': _L0_attn_in['wk'], 'L0_attn_bk': _L0_attn_in['bk'], 'L0_attn_wv': _L0_attn_in['wv'], 'L0_attn_bv': _L0_attn_in['bv'], 'L0_attn_wo': _L0_attn_in['wo'], 'L0_attn_bo': _L0_attn_in['bo'], 'L0_attn_proj_w': _L0_attn_in['proj_w'], 'L0_attn_proj_b': _L0_attn_in['proj_b'], 'L0_ffn_gate_up_proj': _L0_ffn_in['gate_up_proj'], 'L0_ffn_down_proj': _L0_ffn_in['down_proj'], 'L0_ffn_router_w': _L0_ffn_in['router_w']}
    _x0 = _d['L0_attn_x']
    _d['L0_attn_x'] = jax.random.normal(jax.random.fold_in(jax.random.key(seed), 1), (2, 2048, 256), dtype=_x0.dtype)
    del _x0
    return _d

def reference(L0_attn_x, L0_attn_conv_w, L0_attn_conv_b, L0_attn_wq, L0_attn_bq, L0_attn_wk, L0_attn_bk, L0_attn_wv, L0_attn_bv, L0_attn_wo, L0_attn_bo, L0_attn_proj_w, L0_attn_proj_b, L0_ffn_gate_up_proj, L0_ffn_down_proj, L0_ffn_router_w):

    def _L0_attn_ref(x, conv_w, conv_b, wq, bq, wk, bk, wv, bv, wo, bo, proj_w, proj_b):
        import jax, jax.numpy as jnp
        import numpy as np
        from jax import lax
        BLOCKS = 16
        NUM_HEADS = 8
        KEY_DIM = 64
        WIDTH = 64
        D_MODEL = 256

        def _forward(x, conv_w, conv_b, wq, bq, wk, bk, wv, bv, wo, bo, proj_w, proj_b):
            N, T, D = x.shape
            xp = jnp.pad(x, ((0, 0), (2, 0), (0, 0)))
            qkv = lax.conv_general_dilated(xp, conv_w, window_strides=(1,), padding='VALID', dimension_numbers=('NWC', 'WIO', 'NWC')) + conv_b
            q, k, v = jnp.split(qkv, 3, axis=-1)
            block_len = T // BLOCKS
            qb = q.reshape(N * BLOCKS, block_len, WIDTH)
            kb = k.reshape(N * BLOCKS, block_len, WIDTH)
            vb = v.reshape(N * BLOCKS, block_len, WIDTH)
            qh = jnp.einsum('bsd,dhk->bshk', qb, wq) + bq
            kh = jnp.einsum('bsd,dhk->bshk', kb, wk) + bk
            vh = jnp.einsum('bsd,dhk->bshk', vb, wv) + bv
            scale = 1.0 / jnp.sqrt(jnp.asarray(KEY_DIM, qh.dtype))
            scores = jnp.einsum('bqhk,bshk->bhqs', qh * scale, kh)
            causal = jnp.tril(jnp.ones((block_len, block_len), bool))
            scores = jnp.where(causal[None, None], scores, jnp.asarray(-1000000000.0, scores.dtype))
            attn = jax.nn.softmax(scores, axis=-1)
            ctx = jnp.einsum('bhqs,bshk->bqhk', attn, vh)
            mha_out = jnp.einsum('bqhk,hko->bqo', ctx, wo) + bo
            mha_out = mha_out.reshape(N, T, WIDTH)
            out = mha_out @ proj_w + proj_b
            return out
        return _forward(x, conv_w, conv_b, wq, bq, wk, bk, wv, bv, wo, bo, proj_w, proj_b)

    def _L0_ffn_ref(x, gate_up_proj, down_proj, router_w):
        import jax, jax.numpy as jnp
        import numpy as np
        from jax import lax
        TOP_K = 2
        NORM_TOPK = True
        W_SCALE = 0.02
        B, S, D = x.shape
        E = gate_up_proj.shape[0]
        h = x.reshape(-1, D)
        T = h.shape[0]
        logits = h @ router_w.T
        probs = jax.nn.softmax(logits.astype(jnp.float32), axis=-1)
        vals, idx = lax.top_k(probs, TOP_K)
        if NORM_TOPK:
            vals = vals / vals.sum(axis=-1, keepdims=True)
        combine = jnp.zeros((T, E), dtype=probs.dtype)
        combine = combine.at[jnp.arange(T)[:, None], idx].add(vals)

        def step(acc, per_expert):
            gup, dp, cw = per_expert
            gate, up = jnp.split(h @ gup.T, 2, axis=-1)
            y = jax.nn.silu(gate) * up @ dp.T
            return (acc + cw[:, None].astype(acc.dtype) * y, None)
        out, _ = lax.scan(step, jnp.zeros_like(h), (gate_up_proj, down_proj, combine.T))
        return out.reshape(B, S, D)
    x = L0_attn_x
    x = x + 0.5 * _L0_ffn_ref(_layernorm(x, axis=-1), L0_ffn_gate_up_proj, L0_ffn_down_proj, L0_ffn_router_w)
    x = x + _L0_attn_ref(_layernorm(x, axis=-1), L0_attn_conv_w, L0_attn_conv_b, L0_attn_wq, L0_attn_bq, L0_attn_wk, L0_attn_bk, L0_attn_wv, L0_attn_bv, L0_attn_wo, L0_attn_bo, L0_attn_proj_w, L0_attn_proj_b)
    x = x + 0.5 * _L0_ffn_ref(_layernorm(x, axis=-1), L0_ffn_gate_up_proj, L0_ffn_down_proj, L0_ffn_router_w)
    return x

_drawn_inputs = setup_inputs


def setup_inputs(seed=0):
    import zlib

    import numpy as np

    out = dict(_drawn_inputs(seed))
    spreads = {'L0_attn_conv_b': (0.0, 0.434),
     'L0_attn_bq': (0.0, 0.8),
     'L0_attn_bk': (0.0, 0.8),
     'L0_attn_bv': (0.0, 0.1),
     'L0_attn_bo': (0.0, 0.1),
     'L0_attn_proj_b': (0.0, 0.1)}
    factors = {'L0_attn_conv_w': 2.765,
     'L0_attn_wq': 8.0,
     'L0_attn_wk': 8.0,
     'L0_ffn_gate_up_proj': 5.4,
     'L0_ffn_down_proj': 5.086,
     'L0_ffn_router_w': 5.97}
    for name, (base, spread) in spreads.items():
        noise = np.random.default_rng([zlib.crc32(name.encode()), seed]).standard_normal(out[name].shape)
        drawn = base * np.exp(spread * noise) if base else spread * noise
        out[name] = jnp.asarray(drawn.astype(out[name].dtype))
    for name, factor in factors.items():
        out[name] = (out[name] * factor).astype(out[name].dtype)
    return out
```

```python
from contextlib import ExitStack

import numpy as np

import concourse.bass as bass
from concourse import mybir

ALU = mybir.AluOpType
ACT = mybir.ActivationFunctionType
AX = mybir.AxisListType
F32 = mybir.dt.float32
BF16 = mybir.dt.bfloat16
I32 = mybir.dt.int32

P = 128
BATCH, SEQ, D = 2, 2048, 256
TOKENS = BATCH * SEQ
TILES = TOKENS // P
DC = D // P
E, TOPK = 8, 2
H = 176
GU = 2 * H
HC = ((0, P), (P, H - P))
SLOT_TILES = (TOPK * TOKENS + E * (P - 1)) // P
SLOT_TILES += SLOT_TILES % 2
TAPS, W = 3, 64
NH, KD = 8, 64
SCALE = float(KD) ** -0.5
HEAD_AT = [4 * (h % 2) + h // 2 for h in range(NH)]
GROUP = 8
GROUPS = TILES // GROUP
EPS = 1e-5
MAGIC = 12582912.0
RSQRT_SEED = float(0x5F3759DF)
MASKED = -1e9


class Steps:

    def __init__(self, eng, sem):
        self.eng, self.sem, self.n, self.loop = eng, sem, 0, 0

    def did(self, instruction):
        instruction.then_inc(self.sem, 1)
        self.n += 1

    def wait(self):
        self.eng.wait_ge(self.sem, self.loop + self.n)

    def enter(self, var, per_round):
        self.n0, self.per_round = self.n, per_round
        self.loop = var * per_round

    def leave(self, rounds):
        assert self.n == self.n0 + self.per_round, (self.n - self.n0, self.per_round)
        self.n, self.loop = self.n0 + rounds * self.per_round, 0


def macaron_kernel(nc, x, conv_w, conv_b, wq, wk, wvT, wo, bq, bk, bo, proj_w, proj_b, gupT, dpT, rwT,
                   out, h_dram, y_dram):
    ctx = ExitStack()
    with ctx:
        def sb(name, shape, dt=F32):
            return ctx.enter_context(nc.sbuf_tensor(name, shape, dt))

        def pb(name, banks):
            return ctx.enter_context(nc.psum_tensor(name, [P, 512 * banks], F32))

        def sem(name):
            return ctx.enter_context(nc.semaphore(name))

        x_sb = sb("x_sb", [P, TILES * D])
        h_sb = sb("h_sb", [P, TILES * D])
        gup_sb = sb("gup_sb", [P, E * DC * GU])
        dp_sb = sb("dp_sb", [P, E * 2 * D])
        rw_sb = sb("rw_sb", [P, DC * E])
        conv_sb = sb("conv_sb", [P, TAPS * DC, 3 * W])
        convb_sb = sb("convb_sb", [P, 2])
        wq_sb = sb("wq_sb", [W + 1, NH * KD])
        wk_sb = sb("wk_sb", [W + 1, NH * KD])
        wvT_sb = sb("wvT_sb", [KD, NH, W + 1])
        wo_sb = sb("wo_sb", [KD, NH, W])
        vo_sb = sb("vo_sb", [W + 1, NH * W])
        bo_sb = sb("bo_sb", [W, 1])
        proj_sb = sb("proj_sb", [W + 1, D])
        ident = sb("ident", [P, P])
        ident_bf = sb("ident_bf", [P, P], BF16)
        before_bf = sb("before_bf", [P, P], BF16)
        ones_bf = sb("ones_bf", [P, P], BF16)
        mask_bf = sb("mask_bf", [P, 4 * P], BF16)
        iota_i = sb("iota_i", [P, P], I32)
        iota_f = sb("iota_f", [P, P])
        iota_bf = sb("iota_bf", [P, P], BF16)
        part_i = sb("part_i", [P, 1], I32)
        part_f = sb("part_f", [P, 1])
        erank = sb("erank", [P, E])
        zeros = sb("zeros", [P, TILES * E])
        keep = sb("keep", [P, TILES])
        stats = sb("stats", [P, GROUP, 6])
        mv = sb("mv", [P, GROUP, 2])
        var = sb("var", [P, GROUP])
        rstd = sb("rstd", [P, GROUP])
        nt = sb("nt", [P, GROUP])
        hT_sb = sb("hT_sb", [P, 2, D])
        lg = sb("lg", [P, TILES, E])
        lg2 = sb("lg2", [P, TILES, E])
        tmp = sb("tmp", [P, TILES, E])
        top = sb("top", [P, TOPK, TILES])
        pick = sb("pick", [P, TOPK, TILES])
        oh = sb("oh", [P, TOPK, TILES, E])
        sel_bf = sb("sel_bf", [P, TILES * E], BF16)
        wts = sb("wts", [P, TOPK, TILES])
        wtmp = sb("wtmp", [P, 2, TILES])
        tot = sb("tot", [P, E, TILES])
        cum = sb("cum", [P, E, TILES])
        ecnt = sb("ecnt", [P, E])
        etil = sb("etil", [P, E])
        etcum = sb("etcum", [P, E])
        eadj = sb("eadj", [P, E])
        slot = sb("slot", [P, TOPK, TILES])
        stile = sb("stile", [P, TOPK, TILES])
        slane = sb("slane", [P, TOPK, TILES])
        slot_i = sb("slot_i", [P, TOPK, TILES], I32)
        eidw = sb("eidw", [1, SLOT_TILES, E])
        eidf = sb("eidf", [1, SLOT_TILES])
        eid_i = sb("eid_i", [1, SLOT_TILES], I32)
        lane_oh = sb("lane_oh", [P, 2, TOPK, P], BF16)
        tile_oh = sb("tile_oh", [P, 2, TOPK, 2 * SLOT_TILES], BF16)
        tokf = sb("tokf", [P, SLOT_TILES])
        tok_i = sb("tok_i", [P, SLOT_TILES], I32)
        RING = 4
        stage = sb("stage", [P, 2, RING], I32)
        rows = sb("rows", [P, RING, D])
        rowsT = sb("rowsT", [P, 2, D])
        gate = sb("gate", [P, 2, H])
        hid = sb("hid", [P, 2, H])
        hidT = sb("hidT", [P, 2, 2 * P])
        y_sb = sb("y_sb", [P, RING, D])
        cstage = sb("cstage", [P, 2, TOPK], I32)
        yg = sb("yg", [P, 2, TOPK, D])
        xT = sb("xT", [P, 2, DC, P + TAPS - 1])
        qT = sb("qT", [W + 1, P])
        kT = sb("kT", [W + 1, P])
        vT = sb("vT", [W + 1, P])
        qh = sb("qh", [P, 512])
        kh = sb("kh", [P, 512])
        vo = sb("vo", [P, 2, 512])
        nmax = sb("nmax", [P, 2, NH])
        psums = sb("psums", [P, 2, NH])
        prec = sb("prec", [P, 2, NH])
        pr = sb("pr", [P, 2, NH, P])
        prT = sb("prT", [P, NH, P])
        mha = sb("mha", [P, W])
        mhaT = sb("mhaT", [W + 1, P])
        h_now = sb("h_now", [P, 2, D])

        A = pb("A", 1)
        B = pb("B", 1)
        CC = pb("CC", 2)
        F = pb("F", 1)
        SS = pb("SS", 2)
        G = pb("G", 1)

        loaded = sem("loaded")
        made = sem("made")
        const = sem("const")
        phase = sem("phase")
        dve = sem("dve")
        act = sem("act")
        wprep = sem("wprep")
        Z = [{n: sem(f"{n}{k}") for n in names.split()} for k, names in enumerate((
            "normed staged transposed copied stored", "normed g0 g1 combined gate",
            "normed staged transposed copied stored", "g0 g1 combined gate"))]
        R = [dict() for _ in range(2)]
        for L in range(2):
            for n in ("logits", "picked", "diff", "expd", "counted", "onehot", "tabled", "table", "gate_pool",
                      "staged", "g0", "g1", "g2", "g3", "rowsT", "rowsT_sb", "gu", "silu", "hid", "hidT", "hidT_sb",
                      "y", "y_sb", "st0", "st1", "st2", "st3"):
                R[L][n] = sem(f"r{L}_{n}")
        T = {n: sem(f"a_{n}") for n in ("h_now", "xT", "xT_sb", "halo", "qkv", "qkv_sb", "proj3", "qh_sb", "kh_sb", "vo_sb", "scores",
                                        "max", "exp", "norm", "prT", "prT_a", "prT_d", "mha", "mha_sb", "mhaT",
                                        "mhaT_sb", "out", "res")}
        written = sem("written")
        final = sem("final")
        passed_dve = sem("passed_dve")
        passed_pe = sem("passed_pe")
        ENGINES = 5

        block = ctx.enter_context(nc.Block())
        x_rows = x.rearrange("b s d -> (b s) d").rearrange("(i p) d -> p i d", p=P)
        out_rows = out.rearrange("b s d -> (b s) d").rearrange("(i p) d -> p i d", p=P)
        x_view = x_sb[:, :].rearrange("p (i d) -> p i d", d=D)
        dp_view = dp_sb[:, :].rearrange("p (e c d) -> p e c d", c=2, d=D)
        loads = [(x_view[:, g * GROUP:(g + 1) * GROUP, :], x_rows[:, g * GROUP:(g + 1) * GROUP, :])
                 for g in range(GROUPS)]
        loads += [(rw_sb[:, :], rwT), (gup_sb[:, :], gupT)]
        loads += [(dp_view[0:w, :, c, :], dpT[o:o + w, :, :]) for c, (o, w) in enumerate(HC)]
        loads += [(conv_sb[:, :, :], conv_w), (convb_sb[:, 0:1], conv_b[0:2 * W, :]),
                  (convb_sb[0:W, 1:2], conv_b[2 * W:3 * W, :]), (wq_sb[0:W, :], wq), (wq_sb[W:W + 1, :], bq),
                  (wk_sb[0:W, :], wk), (wk_sb[W:W + 1, :], bk), (wvT_sb[:, :, :], wvT),
                  (wo_sb[:, :, :], wo), (bo_sb[:, :], bo), (proj_sb[0:W, :], proj_w), (proj_sb[W:W + 1, :], proj_b)]
        N_CONST = 10 + BATCH + 4

        zeros_bf = zeros[:, :].bitcast(BF16)

        def x_tile(t):
            return x_sb[:, bass.ds(t * D, D)]

        def h_tile(t):
            return h_sb[:, bass.ds(t * D, D)]

        def end_phase(eng, k):
            eng.drain().then_inc(phase, 1)
            eng.wait_ge(phase, ENGINES * (k + 1))

        @block.sync
        def _(sp):
            for dst, src in loads:
                sp.dma_start(dst, src).then_inc(loaded, 16)

            def store_h(L):
                z = Z[L]
                with sp.Fori(0, GROUPS) as g:
                    sp.wait_ge(z["normed"], GROUP * (g + 1))
                    sp.dma_start(h_dram[bass.ds(g * GROUP * P, GROUP * P), :].rearrange("(i p) d -> p i d", p=P),
                                 h_sb[:, bass.ds(g * GROUP * D, GROUP * D)].rearrange("p (i d) -> p i d", d=D)
                                 ).then_inc(z["stored"], 16)
                sp.wait_ge(z["stored"], 16 * GROUPS)

            def store_y(L):
                r = R[L]
                for u in range(RING):
                    sp.sem_inc(r[f"st{u}"], 16)
                with sp.Fori(0, SLOT_TILES // RING) as j:
                    for u in range(RING):
                        sp.wait_ge(r["y_sb"], RING * j + u + 1 + 2)
                        sp.dma_start(y_dram[bass.ds((RING * j + u) * P, P), :], y_sb[:, u, :]
                                     ).then_inc(r[f"st{u}"], 16)
                for u in range(RING):
                    sp.wait_ge(r[f"st{u}"], 16 * (SLOT_TILES // RING + 1))

            ph = 0
            for L in range(2):
                store_h(2 * L)
                end_phase(sp, ph)
                end_phase(sp, ph + 1)
                store_y(L)
                end_phase(sp, ph + 2)
                if L == 0:
                    end_phase(sp, ph + 3)
                    end_phase(sp, ph + 4)
                ph += 5
            with sp.Fori(0, GROUPS) as g:
                sp.wait_ge(final, GROUP * (g + 1))
                sp.dma_start(out_rows[:, bass.ds(g * GROUP, GROUP), :], x_view[:, bass.ds(g * GROUP, GROUP), :]
                             ).then_inc(written, 16)
            sp.wait_ge(written, 16 * GROUPS)

        @block.gpsimd
        def _(pool):
            made_n = [0]

            def const_step(ins):
                ins.then_inc(made, 1)
                made_n[0] += 1
                pool.wait_ge(made, made_n[0])

            const_step(pool.memset(ident[:, :], 0.0))
            const_step(pool.affine_select(out=ident[:, :], in_=ident[:, :], compare_op=ALU.not_equal, fill=1.0,
                                          base=0, pattern=[[-1, P]], channel_multiplier=1))
            const_step(pool.memset(ones_bf[:, :], 1.0))
            const_step(pool.affine_select(out=before_bf[:, :], in_=ones_bf[:, :], compare_op=ALU.is_gt, fill=0.0,
                                          base=0, pattern=[[1, P]], channel_multiplier=-1))
            const_step(pool.memset(mask_bf[:, :], 0.0))
            const_step(pool.affine_select(out=mask_bf[:, :].rearrange("p (h s) -> p h s", s=P),
                                          in_=mask_bf[:, :].rearrange("p (h s) -> p h s", s=P),
                                          compare_op=ALU.is_ge, fill=MASKED,
                                          base=0, pattern=[[0, 4], [-1, P]], channel_multiplier=1))
            const_step(pool.iota(iota_i[:, :], pattern=[[1, P]], base=0, channel_multiplier=0))
            const_step(pool.iota(part_i[:, :], pattern=[[0, 1]], base=0, channel_multiplier=1))
            const_step(pool.memset(zeros[:, :], 0.0))
            const_step(pool.memset(keep[:, :], 1.0))
            for b in range(1, BATCH + 1):
                last = b * TILES // BATCH - 1
                const_step(pool.memset(keep[:, last:last + 1], 0.0))
            for t in (qT, kT, vT, mhaT):
                const_step(pool.memset(t[W:W + 1, :], 1.0))
            assert made_n[0] == N_CONST

            def gather_rows(L):
                r = R[L]
                half = 2 * RING
                with pool.Fori(0, SLOT_TILES // half) as j:
                    for k in range(2):
                        pool.wait_ge(r["rowsT"], (2 * j + k) * RING + 1)
                        ids = tok_i[:, bass.ds((2 * j + k) * RING, RING)]
                        pool.tensor_copy(stage[:, k, :], ids).then_inc(r["staged"], 1)
                        pool.wait_ge(r["staged"], 2 * j + k + 1)
                        for u in range(RING):
                            pool.wait_ge(r["rowsT"], (2 * j + k) * RING + u + 1)
                            pool.sem_inc(r["gate_pool"], 1)
                            pool.indirect_dma_start(
                                out=rows[:, u, :], out_offset=None, in_=h_dram[:, :],
                                in_offset=bass.IndirectOffsetOnAxis(ap=stage[:, k, u:u + 1], axis=0)
                            ).then_inc(r[f"g{u}"], 16)

            def gather_pairs(L, z):
                r = R[L]
                with pool.Fori(0, TILES // 2) as j:
                    for p in range(2):
                        pool.wait_ge(z["combined"], 2 * j + p + 1)
                        pool.tensor_copy(cstage[:, p, :], slot_i[:, :, bass.ds(2 * j + p, 1)]
                                         .rearrange("p k a -> p (k a)")).then_inc(r["staged"], 1)
                        pool.wait_ge(r["staged"], SLOT_TILES // RING + 2 * j + p + 1)
                        pool.sem_inc(z["gate"], 1)
                        for k in range(TOPK):
                            pool.indirect_dma_start(
                                out=yg[:, p, k, :], out_offset=None, in_=y_dram[:, :],
                                in_offset=bass.IndirectOffsetOnAxis(ap=cstage[:, p, k:k + 1], axis=0)
                            ).then_inc(z[f"g{p}"], 16)

            ph = 0
            for L in range(2):
                z = Z[2 * L]
                with pool.Fori(0, TILES // 2) as j:
                    for p in range(2):
                        pool.wait_ge(z["normed"], 2 * j + p + 1)
                        pool.wait_ge(z["transposed"], 2 * j + p + 1)
                        pool.tensor_copy(h_now[:, p, :], h_tile(2 * j + p)).then_inc(z["staged"], 1)
                end_phase(pool, ph)
                end_phase(pool, ph + 1)
                gather_rows(L)
                end_phase(pool, ph + 2)
                gather_pairs(L, Z[2 * L + 1])
                if L == 0:
                    end_phase(pool, ph + 3)
                    with pool.Fori(0, TILES // 2) as j:
                        for p in range(2):
                            pool.wait_ge(T["xT"], 2 * j + p + 1)
                            pool.tensor_copy(h_now[:, p, :], h_tile(2 * j + p)).then_inc(T["h_now"], 1)
                            pool.wait_ge(T["exp"], 2 * j + p + 1)
                            pool.wait_ge(T["max"], 2 * (2 * j + p + 1) )
                            pool.tensor_tensor(pr[:, p, :, :], pr[:, p, :, :],
                                               prec[:, p, :].unsqueeze(2).to_broadcast([P, NH, P]),
                                               ALU.mult).then_inc(T["norm"], 1)
                    end_phase(pool, ph + 4)
                ph += 5

        @block.scalar
        def _(a):
            a.wait_ge(wprep, 1)
            a.activation(vo_sb[:, :], A[0:W + 1, :], ACT.Copy).then_inc(wprep, 1)

            def copy_hT(z):
                a.sem_inc(z["copied"], 2)
                with a.Fori(0, TILES // 2) as j:
                    for p in range(2):
                        a.wait_ge(z["transposed"], 2 * j + p + 1 + 2)
                        a.activation(hT_sb[:, p, :], (A, B)[p][:, 0:D], ACT.Copy).then_inc(z["copied"], 1)

            def experts(r):
                a.sem_inc(r["rowsT_sb"], 2)
                a.sem_inc(r["y_sb"], 2)

                def silu_s(p, s):
                    a.wait_ge(r["gu"], s + 1 + 2)
                    a.wait_ge(r["hid"], s + 1)
                    a.activation(gate[:, p, :], CC[:, 512 * p:512 * p + H], ACT.Silu).then_inc(r["silu"], 1)

                def rowsT_s(p, s):
                    a.wait_ge(r["rowsT"], s + 1 + RING)
                    a.wait_ge(r["gu"], s + 1)
                    a.activation(rowsT[:, p, :], (A, B)[p][:, 0:D], ACT.Copy).then_inc(r["rowsT_sb"], 1)

                def y_s(u, s, round_):
                    a.wait_ge(r["y"], s + 1 + 2)
                    a.wait_ge(r[f"st{u % RING}"], 16 * (round_ + 1))
                    a.activation(y_sb[:, u % RING, :], SS[:, 512 * (u % 2):512 * (u % 2) + D], ACT.Copy
                                 ).then_inc(r["y_sb"], 1)

                rowsT_s(0, 0)
                rowsT_s(1, 1)
                silu_s(0, 0)
                NB = (SLOT_TILES - 4) // RING
                with a.Fori(0, NB) as j:
                    for u in range(1, 5):
                        s = RING * j + u
                        rowsT_s((u + 1) % 2, s + 1)
                        silu_s(u % 2, s)
                        y_s(u - 1, s - 1, j)
                for s in range(RING * NB + 1, SLOT_TILES + 1):
                    if s + 1 < SLOT_TILES:
                        rowsT_s((s + 1) % 2, s + 1)
                    if s < SLOT_TILES:
                        silu_s(s % 2, s)
                    y_s(s - 1, s - 1, (s - 1) // RING)

            def attention():
                t = T
                with a.Fori(0, TILES // 2) as j:
                    for p in range(2):
                        b = 2 * j + p
                        a.wait_ge(t["xT"], b + 1 + 2)
                        a.wait_ge(t["qkv"], b + 1)
                        a.wait_ge(t["halo"], b + 1)
                        a.activation(xT[:, p, :, TAPS - 1:], A[:, 0:D].rearrange("p (c n) -> p c n", c=DC),
                                     ACT.Copy).then_inc(t["xT_sb"], 1)
                        a.wait_ge(t["proj3"], 3 * b + 1)
                        a.activation(qh[:, :], CC[:, 0:512], ACT.Copy, scale=SCALE).then_inc(t["qh_sb"], 1)
                        a.wait_ge(t["proj3"], 3 * b + 3)
                        a.wait_ge(t["mha"], b + 1)
                        a.activation(vo[:, p, :], F[:, :], ACT.Copy).then_inc(t["vo_sb"], 1)
                        for h in range(NH):
                            if h == 0:
                                a.wait_ge(t["max"], 2 * b + 1)
                                a.wait_ge(t["prT"], b + 1)
                            i = a.activation(pr[:, p, h, :], SS[:, h * P:(h + 1) * P], ACT.Exp,
                                             bias=nmax[:, p, h:h + 1], accum_out=psums[:, p, h:h + 1])
                        i.then_inc(t["exp"], 1)
                        a.wait_ge(t["prT"], b + 1 + 2)
                        a.activation(prT[:, 0:4, :], CC[:, 0:512].rearrange("p (h n) -> p h n", h=4),
                                     ACT.Copy).then_inc(t["prT_a"], 1)

            ph = 0
            for L in range(2):
                copy_hT(Z[2 * L])
                end_phase(a, ph)
                a.wait_ge(R[L]["diff"], 1)
                a.activation(wtmp[:, 0, :], wtmp[:, 1, :], ACT.Exp).then_inc(R[L]["expd"], 1)
                end_phase(a, ph + 1)
                experts(R[L])
                end_phase(a, ph + 2)
                if L == 0:
                    end_phase(a, ph + 3)
                    attention()
                    end_phase(a, ph + 4)
                ph += 5

        @block.vector
        def _(v):
            st = Steps(v, dve)
            v.wait_ge(made, N_CONST)
            v.wait_ge(loaded, 16 * len(loads))
            v.tensor_copy(ident_bf[:, :], ident[:, :]).then_inc(const, 1)
            v.tensor_copy(iota_f[:, :], iota_i[:, :]).then_inc(const, 1)
            v.tensor_copy(iota_bf[:, :], iota_i[:, :]).then_inc(const, 1)
            v.tensor_copy(part_f[:, :], part_i[:, :]).then_inc(const, 1)
            v.wait_ge(const, 4)
            v.tensor_scalar(erank[:, :], iota_f[:, 0:E], -float(E), None, ALU.add).then_inc(const, 1)
            v.wait_ge(const, 5)

            def normalise(z, combine, norm):
                per = (TOPK * GROUP if combine else 0) + (2 * GROUP + 12 if norm else 0)
                if combine:
                    v.sem_inc(z["combined"], 2)
                with v.Fori(0, GROUPS) as g:
                    st.enter(g, per)
                    for u in range(GROUP):
                        t = GROUP * g + u
                        if combine:
                            v.wait_ge(z[f"g{u % 2}"], 16 * TOPK * ((GROUP // 2) * g + u // 2 + 1))
                            for k in range(TOPK):
                                i = v.scalar_tensor_tensor(out=x_tile(t), in0=yg[:, u % 2, k, :],
                                                           scalar=wts[:, k, bass.ds(t, 1)], in1=x_tile(t),
                                                           op0=ALU.mult, op1=ALU.add)
                                st.did(i)
                                st.wait()
                            v.sem_inc(z["combined"], 1)
                            if not norm:
                                v.sem_inc(final, 1)
                        if norm:
                            st.did(v.bn_stats(stats[:, u, :], x_tile(t)))
                    if norm:
                        st.wait()
                        v.sem_inc(passed_dve, 1)
                        for u in range(GROUP):
                            st.did(v.bn_aggr(mv[:, u, :], stats[:, u, :]))
                        st.wait()
                        st.did(v.tensor_scalar(var[:, :], mv[:, :, 1], EPS, None, ALU.add))
                        st.wait()
                        st.did(v.tensor_scalar(nt[:, :].bitcast(I32), var[:, :].bitcast(I32), 1, None,
                                               ALU.logical_shift_right))
                        st.wait()
                        st.did(v.tensor_scalar(rstd[:, :].bitcast(I32), nt[:, :].bitcast(I32), -1.0, RSQRT_SEED,
                                               ALU.mult, ALU.add))
                        st.wait()
                        for _ in range(3):
                            st.did(v.tensor_tensor(nt[:, :], rstd[:, :], rstd[:, :], ALU.mult))
                            st.wait()
                            st.did(v.scalar_tensor_tensor(out=nt[:, :], in0=nt[:, :], scalar=-0.5, in1=var[:, :],
                                                          op0=ALU.mult, op1=ALU.mult))
                            st.wait()
                            st.did(v.scalar_tensor_tensor(out=rstd[:, :], in0=nt[:, :], scalar=1.5, in1=rstd[:, :],
                                                          op0=ALU.add, op1=ALU.mult))
                            st.wait()
                        for u in range(GROUP):
                            v.tensor_scalar(h_tile(GROUP * g + u), x_tile(GROUP * g + u), mv[:, u, 0:1],
                                            rstd[:, u:u + 1], ALU.subtract, ALU.mult).then_inc(z["normed"], 1)
                st.leave(GROUPS)

            def route(L):
                r = R[L]

                def step(i):
                    st.did(i)
                    st.wait()

                def over_e(ap):
                    return ap.unsqueeze(2).to_broadcast([P, TILES, E])

                step(v.tensor_copy(lg[:, :, :], F[:, 0:TILES * E].rearrange("p (i e) -> p i e", e=E)))
                src = lg
                ranks = erank[:, :].unsqueeze(1).to_broadcast([P, TILES, E])
                for k in range(TOPK):
                    step(v.tensor_reduce(top[:, k, :], src[:, :, :], AX.X, ALU.max))
                    step(v.tensor_tensor(tmp[:, :, :], src[:, :, :], over_e(top[:, k, :]), ALU.is_equal))
                    step(v.tensor_tensor(tmp[:, :, :], tmp[:, :, :], ranks, ALU.mult))
                    step(v.tensor_reduce(pick[:, k, :], tmp[:, :, :], AX.X, ALU.min))
                    step(v.tensor_tensor(oh[:, k, :, :], over_e(pick[:, k, :]), ranks, ALU.is_equal))
                    if k == 0:
                        step(v.scalar_tensor_tensor(out=lg2[:, :, :], in0=oh[:, 0, :, :], scalar=-3.0e38,
                                                    in1=lg[:, :, :], op0=ALU.mult, op1=ALU.add))
                        src = lg2
                v.tensor_tensor(sel_bf[:, :].rearrange("p (i e) -> p i e", e=E), oh[:, 0, :, :], oh[:, 1, :, :],
                                ALU.add).then_inc(r["picked"], 1)
                v.tensor_tensor(wtmp[:, 1, :], top[:, 1, :], top[:, 0, :], ALU.subtract).then_inc(r["diff"], 1)
                v.wait_ge(r["counted"], 1)
                step(v.tensor_copy(tot[:, :, :], B[:, 0:TILES * E].rearrange("p (i e) -> p e i", e=E)))
                step(v.tensor_tensor_scan(cum[:, :, :].rearrange("p e i -> p (e i)"),
                                          tot[:, :, :].rearrange("p e i -> p (e i)"), zeros[:, :], 0.0,
                                          ALU.add, ALU.add))
                ends = cum[:, :, TILES - 1]
                step(v.tensor_copy(ecnt[:, 0:1], cum[:, 0, TILES - 1:TILES]))
                step(v.tensor_tensor(ecnt[:, 1:E], cum[:, 1:E, TILES - 1], cum[:, 0:E - 1, TILES - 1], ALU.subtract))
                step(v.tensor_scalar(etil[:, :], ecnt[:, :], P / 2 - 0.5, 1.0 / P, ALU.add, ALU.mult))
                step(v.tensor_scalar(etil[:, :], etil[:, :], MAGIC, MAGIC, ALU.add, ALU.subtract))
                step(v.tensor_tensor_scan(etcum[:, :], etil[:, :], zeros[:, 0:E], 0.0, ALU.add, ALU.add))
                step(v.tensor_tensor(eadj[:, :], etcum[:, :], etil[:, :], ALU.subtract))
                step(v.scalar_tensor_tensor(out=eadj[:, :], in0=eadj[:, :], scalar=float(P), in1=ecnt[:, :],
                                            op0=ALU.mult, op1=ALU.add))
                step(v.tensor_tensor(eadj[:, :], eadj[:, :], ends, ALU.subtract))
                step(v.tensor_tensor(cum[:, :, :], cum[:, :, :], tot[:, :, :], ALU.subtract))
                step(v.tensor_tensor(cum[:, :, :], cum[:, :, :], eadj[:, :].unsqueeze(2).to_broadcast([P, E, TILES]),
                                     ALU.add))
                step(v.tensor_tensor(lg[:, :, :], A[:, 0:TILES * E].rearrange("p (i e) -> p i e", e=E),
                                     cum[:, :, :].rearrange("p e i -> p i e"), ALU.add))
                for k in range(TOPK):
                    step(v.tensor_tensor(tmp[:, :, :], lg[:, :, :], oh[:, k, :, :], ALU.mult))
                    step(v.tensor_reduce(slot[:, k, :], tmp[:, :, :], AX.X, ALU.add))
                step(v.tensor_copy(slot_i[:, :, :], slot[:, :, :]))
                step(v.tensor_scalar(stile[:, :, :], slot[:, :, :], 0.5 - P / 2, 1.0 / P, ALU.add, ALU.mult))
                step(v.tensor_scalar(stile[:, :, :], stile[:, :, :], MAGIC, MAGIC, ALU.add, ALU.subtract))
                step(v.scalar_tensor_tensor(out=slane[:, :, :], in0=stile[:, :, :], scalar=-float(P),
                                            in1=slot[:, :, :], op0=ALU.mult, op1=ALU.add))
                step(v.tensor_tensor(eidw[:, :, :], etcum[0:1, :].unsqueeze(1).to_broadcast([1, SLOT_TILES, E]),
                                     iota_f[0:1, 0:SLOT_TILES].unsqueeze(2).to_broadcast([1, SLOT_TILES, E]),
                                     ALU.is_le))
                step(v.tensor_reduce(eidf[:, :], eidw[:, :, 0:E - 1], AX.X, ALU.add))
                step(v.tensor_copy(eid_i[:, :], eidf[:, :]))
                v.wait_ge(r["expd"], 1)
                step(v.tensor_scalar(wtmp[:, 1, :], wtmp[:, 0, :], 1.0, None, ALU.add))
                step(v.reciprocal(wtmp[:, 1, :], wtmp[:, 1, :]))
                step(v.tensor_scalar(wts[:, 0, :], wtmp[:, 1, :], 0.5, None, ALU.mult))
                step(v.tensor_tensor(wts[:, 1, :], wts[:, 0, :], wtmp[:, 0, :], ALU.mult))
                with v.Fori(0, TILES // 2) as j:
                    for p in range(2):
                        i = 2 * j + p
                        v.wait_ge(r["tabled"], i + 1)
                        for k in range(TOPK):
                            col = bass.ds(i, 1)
                            v.tensor_scalar(lane_oh[:, p, k, :], iota_bf[:, :], slane[:, k, col], None, ALU.is_equal)
                            v.tensor_scalar(tile_oh[:, p, k, 0:SLOT_TILES], iota_bf[:, 0:SLOT_TILES],
                                            stile[:, k, col], part_f[:, 0:1], ALU.is_equal, ALU.mult)
                            ins = v.tensor_scalar(tile_oh[:, p, k, SLOT_TILES:], iota_bf[:, 0:SLOT_TILES],
                                                  stile[:, k, col], iota_f[:, col], ALU.is_equal, ALU.mult)
                        ins.then_inc(r["onehot"], 1)
                v.wait_ge(r["table"], 1)
                step(v.tensor_scalar(tokf[:, :], G[:, SLOT_TILES:2 * SLOT_TILES], float(P), None, ALU.mult))
                step(v.tensor_tensor(tokf[:, :], tokf[:, :], G[:, 0:SLOT_TILES], ALU.add))
                step(v.tensor_copy(tok_i[:, :], tokf[:, :]))

            def experts(r):
                v.sem_inc(r["hid"], 2)
                v.sem_inc(r["hidT_sb"], 2)

                def hid_s(p, s):
                    v.wait_ge(r["silu"], s + 1)
                    v.wait_ge(r["hidT"], s + 1)
                    v.tensor_tensor(hid[:, p, :], gate[:, p, :], CC[:, 512 * p + H:512 * p + GU], ALU.mult
                                    ).then_inc(r["hid"], 1)

                def hidT_s(p, s):
                    v.wait_ge(r["hidT"], s + 1 + 2)
                    v.wait_ge(r["y"], s + 1)
                    v.tensor_copy(hidT[:, p, 0:P], (F, G)[p][:, 0:P])
                    v.tensor_copy(hidT[0:H - P, p, P:2 * P], (F, G)[p][0:H - P, P:2 * P]).then_inc(r["hidT_sb"], 1)

                hid_s(0, 0)
                NB = (SLOT_TILES - 4) // RING
                with v.Fori(0, NB) as j:
                    for u in range(1, 5):
                        s = RING * j + u
                        hidT_s((u - 1) % 2, s - 1)
                        hid_s(u % 2, s)
                for s in range(RING * NB + 1, SLOT_TILES + 1):
                    hidT_s((s - 1) % 2, s - 1)
                    if s < SLOT_TILES:
                        hid_s(s % 2, s)

            def attention():
                t = T
                per = 2
                v.sem_inc(t["halo"], 2)
                with v.Fori(0, TILES // 2) as j:
                    st.enter(j, 2 * per)
                    for p in range(2):
                        b = 2 * j + p
                        v.wait_ge(t["xT_sb"], b + 1)
                        v.wait_ge(t["qkv"], b + 2)
                        v.tensor_scalar(xT[:, 1 - p, :, 0:TAPS - 1], xT[:, p, :, P:P + TAPS - 1], keep[:, bass.ds(b, 1)],
                                        None, ALU.mult).then_inc(t["halo"], 1)
                        v.wait_ge(t["qkv"], b + 1 + 2)
                        v.tensor_scalar(qT[0:W, :], B[0:W, 0:P], convb_sb[0:W, 0:1], None, ALU.add)
                        v.tensor_scalar(kT[0:W, :], B[W:2 * W, 0:P], convb_sb[W:2 * W, 0:1], None, ALU.add)
                        v.tensor_scalar(vT[0:W, :], B[0:W, P:2 * P], convb_sb[0:W, 1:2], None, ALU.add
                                        ).then_inc(t["qkv_sb"], 1)
                        v.wait_ge(t["proj3"], 3 * b + 2)
                        v.tensor_copy(kh[:, :], CC[:, 512:1024]).then_inc(t["kh_sb"], 1)
                        v.wait_ge(t["scores"], b + 1)
                        st.did(v.tensor_reduce(nmax[:, p, :], SS[:, :].rearrange("p (h s) -> p h s", s=P), AX.X, ALU.max))
                        st.wait()
                        v.tensor_scalar(nmax[:, p, :], nmax[:, p, :], -1.0, None, ALU.mult).then_inc(t["max"], 1)
                        v.wait_ge(t["exp"], b + 1)
                        v.reciprocal(prec[:, p, :], psums[:, p, :]).then_inc(t["max"], 1)
                        v.wait_ge(t["prT"], b + 1 + 2)
                        v.tensor_copy(prT[:, 4:8, :], CC[:, 512:1024].rearrange("p (h n) -> p h n", h=4)
                                      ).then_inc(t["prT_d"], 1)
                        v.wait_ge(t["mha"], b + 1 + 2)
                        v.tensor_copy(mha[:, :], G[:, 0:W]).then_inc(t["mha_sb"], 1)
                        v.wait_ge(t["mhaT"], b + 1)
                        v.tensor_scalar(mhaT[0:W, :], G[0:W, P:2 * P], bo_sb[:, 0:1], None, ALU.add
                                        ).then_inc(t["mhaT_sb"], 1)
                        v.wait_ge(t["out"], b + 1)
                        st.did(v.tensor_tensor(x_tile(b), x_tile(b), G[:, 256:256 + D], ALU.add))
                        st.wait()
                        v.sem_inc(t["res"], 1)
                st.leave(TILES // 2)

            ph = 0
            for L in range(2):
                normalise(Z[2 * L], False, True)
                end_phase(v, ph)
                route(L)
                end_phase(v, ph + 1)
                experts(R[L])
                end_phase(v, ph + 2)
                if L == 0:
                    normalise(Z[1], True, True)
                    end_phase(v, ph + 3)
                    v.memset(xT[:, 0, :, 0:TAPS - 1], 0.0).then_inc(const, 1)
                    attention()
                    end_phase(v, ph + 4)
                ph += 5
            normalise(Z[3], True, False)

        @block.tensor
        def _(pe):
            pe.wait_ge(loaded, 16 * len(loads))
            pe.wait_ge(const, 5)
            for h in range(NH):
                i = pe.matmul(A[0:W + 1, h * W:(h + 1) * W], wvT_sb[:, h, :], wo_sb[:, h, :], start=True, stop=True)
            i.then_inc(wprep, 1)
            pe.wait_ge(wprep, 2)

            def router(L):
                z = Z[2 * L]
                pe.sem_inc(z["transposed"], 2)

                def turn(p, t):
                    pe.wait_ge(z["staged"], t + 1)
                    pe.wait_ge(z["copied"], t + 1)
                    for c in range(DC):
                        i = pe.transpose((A, B)[p][:, c * P:(c + 1) * P], h_now[:, p, c * P:(c + 1) * P], ident[:, :])
                    i.then_inc(z["transposed"], 1)

                def logits(p, t):
                    pe.wait_ge(z["copied"], t + 3)
                    for c in range(DC):
                        pe.matmul(F[:, bass.ds(t * E, E)], hT_sb[:, p, c * P:(c + 1) * P], rw_sb[:, c * E:(c + 1) * E],
                                  start=(c == 0), stop=(c == DC - 1))

                turn(0, 0)
                turn(1, 1)
                logits(0, 0)
                with pe.Fori(0, TILES // 2 - 1) as j:
                    for p in range(2):
                        turn(p, 2 * j + 2 + p)
                        logits(1 - p, 2 * j + 1 + p)
                logits(1, TILES - 1)

            def route(L):
                r = R[L]
                pe.wait_ge(r["picked"], 1)
                pe.matmul(A[:, 0:TILES * E], before_bf[:, :], sel_bf[:, :], start=True, stop=True)
                pe.matmul(B[:, 0:TILES * E], ones_bf[:, :], sel_bf[:, :], start=True, stop=True).then_inc(r["counted"], 1)
                n = 2 * SLOT_TILES
                pe.matmul(G[:, 0:n], zeros_bf[:, 0:P], zeros_bf[:, 0:n], start=True, stop=False,
                          skip_group_check=True)
                pe.sem_inc(r["tabled"], 2)
                with pe.Fori(0, TILES // 2) as j:
                    for p in range(2):
                        pe.wait_ge(r["onehot"], 2 * j + p + 1)
                        for k in range(TOPK):
                            i = pe.matmul(G[:, 0:n], lane_oh[:, p, k, :], tile_oh[:, p, k, :], start=False,
                                          stop=False, skip_group_check=True)
                        i.then_inc(r["tabled"], 1)
                pe.matmul(G[:, 0:n], zeros_bf[:, 0:P], zeros_bf[:, 0:n], start=False, stop=True,
                          skip_group_check=True).then_inc(r["table"], 1)

            def experts(r):
                pe.sem_inc(r["rowsT"], RING)
                pe.sem_inc(r["gu"], 2)
                pe.sem_inc(r["hidT"], 2)
                pe.sem_inc(r["y"], 2)

                def expert_of(s):
                    return pe.value_load(eid_i[0:1, bass.ds(s, 1)], min_val=0, max_val=E - 1)

                def turn_rows(u, s, grp):
                    pe.wait_ge(r[f"g{u % RING}"], 16 * (grp + 1))
                    pe.wait_ge(r["rowsT_sb"], s + 1)
                    for c in range(DC):
                        i = pe.transpose((A, B)[u % 2][:, c * P:(c + 1) * P], rows[:, u % RING, c * P:(c + 1) * P],
                                         ident[:, :])
                    i.then_inc(r["rowsT"], 1)

                def gate_up(u, s, e):
                    pe.wait_ge(r["rowsT_sb"], s + 1 + 2)
                    pe.wait_ge(r["hid"], s + 1)
                    for c in range(DC):
                        i = pe.matmul(CC[:, 512 * (u % 2):512 * (u % 2) + GU], rowsT[:, u % 2, c * P:(c + 1) * P],
                                      gup_sb[:, bass.ds(e * (DC * GU) + c * GU, GU)], start=(c == 0), stop=(c == DC - 1))
                    i.then_inc(r["gu"], 1)

                def turn_hid(u, s):
                    pe.wait_ge(r["hid"], s + 1 + 2)
                    pe.wait_ge(r["hidT_sb"], s + 1)
                    for c, (o, w) in enumerate(HC):
                        i = pe.transpose((F, G)[u % 2][0:w, c * P:(c + 1) * P], hid[:, u % 2, o:o + w], ident[:, :])
                    i.then_inc(r["hidT"], 1)

                def down(u, s, e):
                    pe.wait_ge(r["hidT_sb"], s + 1 + 2)
                    pe.wait_ge(r["y_sb"], s + 1)
                    for c, (o, w) in enumerate(HC):
                        i = pe.matmul(SS[:, 512 * (u % 2):512 * (u % 2) + D], hidT[0:w, u % 2, c * P:(c + 1) * P],
                                      dp_sb[0:w, bass.ds(e * (2 * D) + c * D, D)], start=(c == 0), stop=(c == 1))
                    i.then_inc(r["y"], 1)

                def step(u, s, grp_next, last_e):
                    if grp_next is not None:
                        turn_rows(u + 1, s + 1, grp_next)
                    turn_hid(u - 1, s - 1)
                    e = None
                    if not isinstance(s, int) or s < SLOT_TILES:
                        e = expert_of(s)
                        gate_up(u, s, e)
                    down(u - 1, s - 1, last_e)
                    return e

                turn_rows(0, 0, 0)
                turn_rows(1, 1, 0)
                gate_up(0, 0, expert_of(0))
                NB = (SLOT_TILES - 4) // RING
                with pe.Fori(0, NB) as j:
                    e = expert_of(RING * j)
                    for u in range(1, 5):
                        e = step(u, RING * j + u, j + (u + 1) // RING, e)
                e = expert_of(RING * NB)
                for s in range(RING * NB + 1, SLOT_TILES + 1):
                    e = step(s, s, (s + 1) // RING if s + 1 < SLOT_TILES else None, e)

            def attention():
                t = T
                pe.sem_inc(t["xT"], 2)
                pe.sem_inc(t["qkv"], 2)
                pe.sem_inc(t["prT"], 2)
                pe.sem_inc(t["mha"], 2)

                def front(p, b, first=False):
                    if not first:
                        pe.wait_ge(t["xT_sb"], b)
                    pe.wait_ge(t["h_now"], b + 1)
                    for c in range(DC):
                        i = pe.transpose(A[:, c * P:(c + 1) * P], h_now[:, p, c * P:(c + 1) * P], ident[:, :])
                    i.then_inc(t["xT"], 1)
                    pe.wait_ge(t["xT_sb"], b + 1)
                    if not first:
                        pe.wait_ge(t["halo"], b + 2)
                        pe.wait_ge(t["qkv_sb"], b)
                    for o, w, dst in ((0, 2 * W, B[:, 0:P]), (2 * W, W, B[0:W, P:2 * P])):
                        for c in range(DC):
                            for k in range(TAPS):
                                i = pe.matmul(dst, conv_sb[:, k * DC + c, o:o + w], xT[:, p, c, k:k + P],
                                              start=(c == 0 and k == 0), stop=(c == DC - 1 and k == TAPS - 1))
                    i.then_inc(t["qkv"], 1)
                    pe.wait_ge(t["qkv_sb"], b + 1)
                    if not first:
                        pe.wait_ge(t["prT_a"], b)
                        pe.wait_ge(t["prT_d"], b)
                        pe.wait_ge(t["vo_sb"], b)
                    for o, wgt, src in ((0, wq_sb, qT), (512, wk_sb, kT)):
                        for m in range(4):
                            i = pe.matmul(CC[:, o + m * P:o + (m + 1) * P], wgt[:, m * P:(m + 1) * P], src[:, :],
                                          start=True, stop=True)
                        i.then_inc(t["proj3"], 1)
                    pe.matmul(F[:, :], vT[:, :], vo_sb[:, :], start=True, stop=True).then_inc(t["proj3"], 1)
                    pe.wait_ge(t["qh_sb"], b + 1)
                    pe.wait_ge(t["kh_sb"], b + 1)
                    if not first:
                        pe.wait_ge(t["exp"], b)
                    for m in range(2):
                        pe.matmul(SS[:, 512 * m:512 * (m + 1)], ident_bf[:, :], mask_bf[:, :], start=True, stop=False,
                                  skip_group_check=True)
                    for h in range(NH):
                        lo, at, m = KD * (h % 2), HEAD_AT[h], h // 2
                        i = pe.matmul(SS[:, at * P:(at + 1) * P], qh[lo:lo + KD, m * P:(m + 1) * P],
                                      kh[lo:lo + KD, m * P:(m + 1) * P], start=False, stop=(m == 3),
                                      skip_group_check=True)
                    i.then_inc(t["scores"], 1)

                def back(p, b, first=False):
                    pe.wait_ge(t["norm"], b + 1)
                    for h in range(NH):
                        i = pe.transpose(CC[:, h * P:(h + 1) * P], pr[:, p, h, :], ident[:, :])
                    i.then_inc(t["prT"], 1)
                    pe.wait_ge(t["prT_a"], b + 1)
                    pe.wait_ge(t["prT_d"], b + 1)
                    if not first:
                        pe.wait_ge(t["res"], b)
                    for h in range(NH):
                        i = pe.matmul(G[:, 0:W], prT[:, HEAD_AT[h], :], vo[:, p, h * W:(h + 1) * W], start=(h == 0),
                                      stop=(h == NH - 1))
                    i.then_inc(t["mha"], 1)
                    pe.wait_ge(t["mha_sb"], b + 1)
                    pe.sem_inc(passed_pe, 1)
                    pe.transpose(G[0:W, P:2 * P], mha[:, :], ident[:, :]).then_inc(t["mhaT"], 1)
                    pe.wait_ge(t["mhaT_sb"], b + 1)
                    pe.matmul(G[:, 256:256 + D], mhaT[:, :], proj_sb[:, :], start=True, stop=True).then_inc(t["out"], 1)

                front(0, 0, True)
                back(0, 0, True)
                front(1, 1)
                back(1, 1)
                with pe.Fori(0, TILES // 2 - 1) as j:
                    for p in range(2):
                        front(p, 2 * j + 2 + p)
                        back(p, 2 * j + 2 + p)

            ph = 0
            for L in range(2):
                router(L)
                end_phase(pe, ph)
                route(L)
                end_phase(pe, ph + 1)
                experts(R[L])
                end_phase(pe, ph + 2)
                if L == 0:
                    end_phase(pe, ph + 3)
                    pe.wait_ge(const, 6)
                    attention()
                    end_phase(pe, ph + 4)
                ph += 5


def kernel(**inputs):
    import numpy as _np
    import concourse.bacc as _bacc
    from concourse import mybir as _mybir
    from concourse.bass_utils import run_bass_kernel_spmd as _run

    a = {n: _np.asarray(v) for n, v in inputs.items()}
    f32 = {
        "x": a["L0_attn_x"],
        "conv_w": a["L0_attn_conv_w"].reshape(TAPS, DC, P, 3 * W).transpose(2, 0, 1, 3).reshape(P, TAPS * DC, 3 * W),
        "conv_b": a["L0_attn_conv_b"].reshape(3 * W, 1),
        "wq": a["L0_attn_wq"].reshape(W, NH * KD),
        "wk": a["L0_attn_wk"].reshape(W, NH * KD),
        "wvT": _np.concatenate([a["L0_attn_wv"].transpose(2, 1, 0), a["L0_attn_bv"].T.reshape(KD, NH, 1)], 2),
        "wo": a["L0_attn_wo"].transpose(1, 0, 2),
        "bq": a["L0_attn_bq"].reshape(1, NH * KD),
        "bk": a["L0_attn_bk"].reshape(1, NH * KD),
        "bo": a["L0_attn_bo"].reshape(W, 1),
        "proj_w": a["L0_attn_proj_w"],
        "proj_b": a["L0_attn_proj_b"].reshape(1, D),
        "gupT": a["L0_ffn_gate_up_proj"].reshape(E, GU, DC, P).transpose(3, 0, 2, 1).reshape(P, E * DC * GU),
        "dpT": a["L0_ffn_down_proj"].transpose(2, 0, 1),
        "rwT": a["L0_ffn_router_w"].reshape(E, DC, P).transpose(2, 1, 0).reshape(P, DC * E),
    }
    nc = _bacc.Bacc("TRN2", target_bir_lowering=False, num_devices=1)
    arrays, args = {}, []
    for name, v in f32.items():
        v = _np.ascontiguousarray(v)
        arrays[f"in_{name}_dram"] = v
        args.append(nc.dram_tensor(f"in_{name}_dram", v.shape, _mybir.dt.from_np(v.dtype), kind="ExternalInput").ap())
    args.append(nc.dram_tensor("out_0_dram", (BATCH, SEQ, D), F32, kind="ExternalOutput").ap())
    args.append(nc.dram_tensor("h_rows", (TOKENS, D), F32, kind="Internal").ap())
    args.append(nc.dram_tensor("y_rows", (SLOT_TILES * P, D), F32, kind="Internal").ap())
    macaron_kernel(nc, *args)
    r = _run(nc, [arrays], core_ids=[0])
    return r.results[0]["out_0_dram"]
```

```python
from contextlib import ExitStack

import numpy as np

import concourse.bass as bass
from concourse import mybir

ALU = mybir.AluOpType
ACT = mybir.ActivationFunctionType
AX = mybir.AxisListType
F32 = mybir.dt.float32
BF16 = mybir.dt.bfloat16
I32 = mybir.dt.int32

P = 128
BATCH, SEQ, D = 2, 2048, 256
TOKENS = BATCH * SEQ
TILES = TOKENS // P
DC = D // P
E, TOPK = 8, 2
H = 176
GU = 2 * H
HC = ((0, P), (P, H - P))
SLOT_TILES = (TOPK * TOKENS + E * (P - 1)) // P
SLOT_TILES += SLOT_TILES % 2
TAPS, W = 3, 64
NH, KD = 8, 64
SCALE = float(KD) ** -0.5
HEAD_AT = [4 * (h % 2) + h // 2 for h in range(NH)]
PRE, POST = 5, 3
GROUP = 8
GROUPS = TILES // GROUP
EPS = 1e-5
MAGIC = 12582912.0
RSQRT_SEED = float(0x5F3759DF)
MASKED = -1e9


class Steps:

    def __init__(self, eng, sem):
        self.eng, self.sem, self.n, self.loop = eng, sem, 0, 0

    def did(self, instruction):
        instruction.then_inc(self.sem, 1)
        self.n += 1

    def wait(self):
        self.eng.wait_ge(self.sem, self.loop + self.n)

    def enter(self, var, per_round):
        self.n0, self.per_round = self.n, per_round
        self.loop = var * per_round

    def leave(self, rounds):
        assert self.n == self.n0 + self.per_round, (self.n - self.n0, self.per_round)
        self.n, self.loop = self.n0 + rounds * self.per_round, 0


def macaron_kernel(nc, x, conv_w, conv_b, wq, wk, wvT, wo, bq, bk, bo, proj_w, proj_b, gupT, dpT, rwT,
                   out, h_dram, y_dram):
    ctx = ExitStack()
    with ctx:
        def sb(name, shape, dt=F32):
            return ctx.enter_context(nc.sbuf_tensor(name, shape, dt))

        def pb(name, banks):
            return ctx.enter_context(nc.psum_tensor(name, [P, 512 * banks], F32))

        def sem(name):
            return ctx.enter_context(nc.semaphore(name))

        x_sb = sb("x_sb", [P, TILES * D])
        h_ring = sb("h_ring", [P, GROUP, D])
        gup_sb = sb("gup_sb", [P, E * DC * GU])
        dp_sb = sb("dp_sb", [P, E * 2 * D])
        rw_sb = sb("rw_sb", [P, DC * E])
        conv_sb = sb("conv_sb", [P, TAPS * DC, 3 * W])
        convb_sb = sb("convb_sb", [P, 2])
        wq_sb = sb("wq_sb", [W + 1, NH * KD])
        wk_sb = sb("wk_sb", [W + 1, NH * KD])
        wvT_sb = sb("wvT_sb", [KD, NH, W + 1])
        wo_sb = sb("wo_sb", [KD, NH, W])
        vo_sb = sb("vo_sb", [W + 1, NH * W])
        bo_sb = sb("bo_sb", [W, 1])
        proj_sb = sb("proj_sb", [W + 1, D])
        ident = sb("ident", [P, P])
        ident_bf = sb("ident_bf", [P, P], BF16)
        before_bf = sb("before_bf", [P, P], BF16)
        ones_bf = sb("ones_bf", [P, P], BF16)
        mask_bf = sb("mask_bf", [P, 4 * P], BF16)
        iota_i = sb("iota_i", [P, P], I32)
        iota_f = sb("iota_f", [P, P])
        iota_bf = sb("iota_bf", [P, P], BF16)
        part_i = sb("part_i", [P, 1], I32)
        part_f = sb("part_f", [P, 1])
        erank = sb("erank", [P, E])
        zeros = sb("zeros", [P, TILES * E])
        keep = sb("keep", [P, TILES])
        stats = sb("stats", [P, GROUP, 6])
        mv = sb("mv", [P, GROUP, 2])
        var = sb("var", [P, GROUP])
        rstd = sb("rstd", [P, GROUP])
        nt = sb("nt", [P, GROUP])
        hT_sb = sb("hT_sb", [P, 2, D])
        lg = sb("lg", [P, TILES, E])
        lg2 = sb("lg2", [P, TILES, E])
        tmp = sb("tmp", [P, TILES, E])
        top = sb("top", [P, TOPK, TILES])
        pick = sb("pick", [P, TOPK, TILES])
        oh = sb("oh", [P, TOPK, TILES, E])
        sel_bf = sb("sel_bf", [P, TILES * E], BF16)
        wts = sb("wts", [P, TOPK, TILES])
        wtmp = sb("wtmp", [P, 2, TILES])
        tot = sb("tot", [P, E, TILES])
        cum = sb("cum", [P, E, TILES])
        ecnt = sb("ecnt", [P, E])
        etil = sb("etil", [P, E])
        etcum = sb("etcum", [P, E])
        eadj = sb("eadj", [P, E])
        slot = sb("slot", [P, TOPK, TILES])
        stile = sb("stile", [P, TOPK, TILES])
        slane = sb("slane", [P, TOPK, TILES])
        slot_i = sb("slot_i", [P, TOPK, TILES], I32)
        eidw = sb("eidw", [1, SLOT_TILES, E])
        eidf = sb("eidf", [1, SLOT_TILES])
        eid_i = sb("eid_i", [1, SLOT_TILES], I32)
        lane_oh = sb("lane_oh", [P, 2, TOPK, P], BF16)
        tile_oh = sb("tile_oh", [P, 2, TOPK, 2 * SLOT_TILES], BF16)
        tokf = sb("tokf", [P, SLOT_TILES])
        tok_i = sb("tok_i", [P, SLOT_TILES], I32)
        RING = 4
        stage = sb("stage", [P, 2, RING], I32)
        rows = sb("rows", [P, RING, D])
        rowsT = sb("rowsT", [P, 2, D])
        gate = sb("gate", [P, 2, H])
        hid = sb("hid", [P, 2, H])
        hidT = sb("hidT", [P, 2, 2 * P])
        y_sb = sb("y_sb", [P, RING, D])
        cstage = sb("cstage", [P, 2, TOPK], I32)
        yg = sb("yg", [P, 2, TOPK, D])
        xT = sb("xT", [P, 2, DC, P + TAPS - 1])
        qT = sb("qT", [W + 1, P])
        kT = sb("kT", [W + 1, P])
        vT = sb("vT", [W + 1, P])
        qh = sb("qh", [P, 512])
        kh = sb("kh", [P, 512])
        vo = sb("vo", [P, 2, 512])
        nmax = sb("nmax", [P, 2, NH])
        psums = sb("psums", [P, 2, NH])
        prec = sb("prec", [P, 2, NH])
        pr = sb("pr", [P, 2, NH, P])
        prT = sb("prT", [P, NH, P])
        mha = sb("mha", [P, W])
        mhaT = sb("mhaT", [W + 1, P])
        ha = sb("ha", [P, 2, D])
        hr = sb("hr", [P, 2, D])
        mv4 = sb("mv4", [P, 4, 2])

        A = pb("A", 1)
        B = pb("B", 1)
        CC = pb("CC", 2)
        F = pb("F", 1)
        SS = pb("SS", 2)
        G = pb("G", 1)

        loaded = sem("loaded")
        made = sem("made")
        const = sem("const")
        phase = sem("phase")
        dve = sem("dve")
        act = sem("act")
        wprep = sem("wprep")
        first = {n: sem(f"first_{n}") for n in "normed transposed copied stored".split()}
        last = {n: sem(f"last_{n}") for n in "g0 g1 combined gate".split()}
        x_in = [sem(f"x_in{g}") for g in range(GROUPS)]
        R = [dict() for _ in range(2)]
        for L in range(2):
            for n in ("logits", "picked", "diff", "expd", "counted", "onehot", "tabled", "table", "gate_pool",
                      "staged", "g0", "g1", "g2", "g3", "rowsT", "rowsT_sb", "gu", "silu", "hid", "hidT", "hidT_sb",
                      "y", "y_sb", "st0", "st1", "st2", "st3"):
                R[L][n] = sem(f"r{L}_{n}")
        T = {n: sem(f"a_{n}") for n in (
            "g0", "g1", "gate", "stage", "combined", "normed", "xT", "hrT", "xT_sb", "hrT_sb", "halo", "qk", "v",
            "qkv_sb", "qh", "kh", "vh", "qh_sb", "kh_sb", "vo_sb", "scores", "max", "exp", "rec", "norm", "prT",
            "prT_a", "prT_d", "mha", "mha_sb", "mhaT", "mhaT_sb", "out", "logits", "res", "lg", "routed", "stored0", "stored1")}
        written = sem("written")
        rw_in = sem("rw_in")
        final = sem("final")
        passed_dve = sem("passed_dve")
        passed_pe = sem("passed_pe")
        ENGINES = 5

        block = ctx.enter_context(nc.Block())
        x_rows = x.rearrange("b s d -> (b s) d").rearrange("(i p) d -> p i d", p=P)
        out_rows = out.rearrange("b s d -> (b s) d").rearrange("(i p) d -> p i d", p=P)
        x_view = x_sb[:, :].rearrange("p (i d) -> p i d", d=D)
        dp_view = dp_sb[:, :].rearrange("p (e c d) -> p e c d", c=2, d=D)
        loads = [(gup_sb[:, :], gupT)]
        loads += [(dp_view[0:w, :, c, :], dpT[o:o + w, :, :]) for c, (o, w) in enumerate(HC)]
        loads += [(conv_sb[:, :, :], conv_w), (convb_sb[:, 0:1], conv_b[0:2 * W, :]),
                  (convb_sb[0:W, 1:2], conv_b[2 * W:3 * W, :]), (wq_sb[0:W, :], wq), (wq_sb[W:W + 1, :], bq),
                  (wk_sb[0:W, :], wk), (wk_sb[W:W + 1, :], bk), (wvT_sb[:, :, :], wvT),
                  (wo_sb[:, :, :], wo), (bo_sb[:, :], bo), (proj_sb[0:W, :], proj_w), (proj_sb[W:W + 1, :], proj_b)]
        N_CONST = 10 + BATCH + 4

        zeros_bf = zeros[:, :].bitcast(BF16)

        def x_tile(t):
            return x_sb[:, bass.ds(t * D, D)]

        def after(eng, sem, n):
            if not isinstance(n, int) or n > 0:
                eng.wait_ge(sem, n)

        FIRST_TURN, LOOP_FROM, LOOP_TO, LAST_TURN = -PRE - 1, 4, TILES - PRE - 1, TILES + POST

        def turns(eng, turn, chain=None, per=0):
            for i in range(FIRST_TURN, LOOP_FROM):
                turn(i, i % 2)
            with eng.Fori(0, (LOOP_TO - LOOP_FROM) // 2) as j:
                if chain:
                    chain.enter(j, per)
                for u in range(2):
                    turn(LOOP_FROM + 2 * j + u, u)
            if chain:
                chain.leave((LOOP_TO - LOOP_FROM) // 2)
            for i in range(LOOP_TO, LAST_TURN):
                turn(i, i % 2)

        def there(b):
            return not isinstance(b, int) or 0 <= b < TILES

        def end_phase(eng, k):
            eng.drain().then_inc(phase, 1)
            eng.wait_ge(phase, ENGINES * (k + 1))

        @block.sync
        def _(sp):
            for g in range(GROUPS):
                sp.dma_start(x_view[:, g * GROUP:(g + 1) * GROUP, :], x_rows[:, g * GROUP:(g + 1) * GROUP, :]
                             ).then_inc(x_in[g], 16)
                if g == 0:
                    sp.dma_start(rw_sb[:, :], rwT).then_inc(rw_in, 16)
                    for dst, src in loads:
                        sp.dma_start(dst, src).then_inc(loaded, 16)

            def store_first():
                with sp.Fori(0, GROUPS) as g:
                    sp.wait_ge(first["normed"], GROUP * (g + 1))
                    sp.dma_start(h_dram[bass.ds(g * GROUP * P, GROUP * P), :].rearrange("(i p) d -> p i d", p=P),
                                 h_ring[:, :, :]).then_inc(first["stored"], 16)
                sp.wait_ge(first["stored"], 16 * GROUPS)

            def store_second():
                with sp.Fori(0, TILES // 2) as j:
                    for q in range(2):
                        sp.wait_ge(T["routed"], 2 * j + q + 1)
                        sp.dma_start(h_dram[bass.ds((2 * j + q) * P, P), :], hr[:, 1 - q, :]
                                     ).then_inc(T[f"stored{1 - q}"], 16)
                for q in range(2):
                    sp.wait_ge(T[f"stored{q}"], 16 * TILES // 2)

            def store_y(L):
                r = R[L]
                for u in range(RING):
                    sp.sem_inc(r[f"st{u}"], 16)
                with sp.Fori(0, SLOT_TILES // RING) as j:
                    for u in range(RING):
                        sp.wait_ge(r["y_sb"], RING * j + u + 1 + 2)
                        sp.dma_start(y_dram[bass.ds((RING * j + u) * P, P), :], y_sb[:, u, :]
                                     ).then_inc(r[f"st{u}"], 16)
                for u in range(RING):
                    sp.wait_ge(r[f"st{u}"], 16 * (SLOT_TILES // RING + 1))

            store_first()
            end_phase(sp, 0)
            end_phase(sp, 1)
            store_y(0)
            end_phase(sp, 2)
            store_second()
            end_phase(sp, 3)
            end_phase(sp, 4)
            store_y(1)
            end_phase(sp, 5)
            with sp.Fori(0, GROUPS) as g:
                sp.wait_ge(final, GROUP * (g + 1))
                sp.dma_start(out_rows[:, bass.ds(g * GROUP, GROUP), :], x_view[:, bass.ds(g * GROUP, GROUP), :]
                             ).then_inc(written, 16)
            sp.wait_ge(written, 16 * GROUPS)

        @block.gpsimd
        def _(pool):
            made_n = [0]

            def const_step(ins):
                ins.then_inc(made, 1)
                made_n[0] += 1
                pool.wait_ge(made, made_n[0])

            const_step(pool.memset(ident[:, :], 0.0))
            const_step(pool.affine_select(out=ident[:, :], in_=ident[:, :], compare_op=ALU.not_equal, fill=1.0,
                                          base=0, pattern=[[-1, P]], channel_multiplier=1))
            const_step(pool.memset(ones_bf[:, :], 1.0))
            const_step(pool.affine_select(out=before_bf[:, :], in_=ones_bf[:, :], compare_op=ALU.is_gt, fill=0.0,
                                          base=0, pattern=[[1, P]], channel_multiplier=-1))
            const_step(pool.memset(mask_bf[:, :], 0.0))
            const_step(pool.affine_select(out=mask_bf[:, :].rearrange("p (h s) -> p h s", s=P),
                                          in_=mask_bf[:, :].rearrange("p (h s) -> p h s", s=P),
                                          compare_op=ALU.is_ge, fill=MASKED,
                                          base=0, pattern=[[0, 4], [-1, P]], channel_multiplier=1))
            const_step(pool.iota(iota_i[:, :], pattern=[[1, P]], base=0, channel_multiplier=0))
            const_step(pool.iota(part_i[:, :], pattern=[[0, 1]], base=0, channel_multiplier=1))
            const_step(pool.memset(zeros[:, :], 0.0))
            const_step(pool.memset(keep[:, :], 1.0))
            for b in range(1, BATCH + 1):
                edge = b * TILES // BATCH - 1
                const_step(pool.memset(keep[:, edge:edge + 1], 0.0))
            for t in (qT, kT, vT, mhaT):
                const_step(pool.memset(t[W:W + 1, :], 1.0))
            assert made_n[0] == N_CONST

            def gather_rows(L):
                r = R[L]
                half = 2 * RING
                with pool.Fori(0, SLOT_TILES // half) as j:
                    for k in range(2):
                        pool.wait_ge(r["rowsT"], (2 * j + k) * RING + 1)
                        ids = tok_i[:, bass.ds((2 * j + k) * RING, RING)]
                        pool.tensor_copy(stage[:, k, :], ids).then_inc(r["staged"], 1)
                        pool.wait_ge(r["staged"], 2 * j + k + 1)
                        for u in range(RING):
                            pool.wait_ge(r["rowsT"], (2 * j + k) * RING + u + 1)
                            pool.sem_inc(r["gate_pool"], 1)
                            pool.indirect_dma_start(
                                out=rows[:, u, :], out_offset=None, in_=h_dram[:, :],
                                in_offset=bass.IndirectOffsetOnAxis(ap=stage[:, k, u:u + 1], axis=0)
                            ).then_inc(r[f"g{u}"], 16)

            def gather_pairs(L, z):
                r = R[L]
                with pool.Fori(0, TILES // 2) as j:
                    for p in range(2):
                        pool.wait_ge(z["combined"], 2 * j + p + 1)
                        pool.tensor_copy(cstage[:, p, :], slot_i[:, :, bass.ds(2 * j + p, 1)]
                                         .rearrange("p k a -> p (k a)")).then_inc(r["staged"], 1)
                        pool.wait_ge(r["staged"], SLOT_TILES // RING + 2 * j + p + 1)
                        pool.sem_inc(z["gate"], 1)
                        for k in range(TOPK):
                            pool.indirect_dma_start(
                                out=yg[:, p, k, :], out_offset=None, in_=y_dram[:, :],
                                in_offset=bass.IndirectOffsetOnAxis(ap=cstage[:, p, k:k + 1], axis=0)
                            ).then_inc(z[f"g{p}"], 16)

            def attention():
                t = T

                def turn(i, u):
                    if there(i):
                        pool.wait_ge(t["rec"], i + 1)
                        pool.tensor_tensor(pr[:, u, :, :], pr[:, u, :, :],
                                           prec[:, u, :].unsqueeze(2).to_broadcast([P, NH, P]),
                                           ALU.mult).then_inc(t["norm"], 1)
                    b, q = i + PRE + 1, (u + PRE + 1) % 2
                    if there(b):
                        after(pool, t["combined"], b - 1)
                        pool.tensor_copy(cstage[:, q, :], slot_i[:, :, bass.ds(b, 1)].rearrange("p k a -> p (k a)")
                                         ).then_inc(t["stage"], 1)
                        pool.wait_ge(t["stage"], b + 1)
                        pool.sem_inc(t["gate"], 1)
                        for k in range(TOPK):
                            pool.indirect_dma_start(
                                out=yg[:, q, k, :], out_offset=None, in_=y_dram[:, :],
                                in_offset=bass.IndirectOffsetOnAxis(ap=cstage[:, q, k:k + 1], axis=0)
                            ).then_inc(t[f"g{q}"], 16)

                turns(pool, turn)

            end_phase(pool, 0)
            end_phase(pool, 1)
            gather_rows(0)
            end_phase(pool, 2)
            attention()
            end_phase(pool, 3)
            end_phase(pool, 4)
            gather_rows(1)
            end_phase(pool, 5)
            gather_pairs(1, last)

        @block.scalar
        def _(a):
            def experts(r):
                a.sem_inc(r["rowsT_sb"], 2)
                a.sem_inc(r["y_sb"], 2)

                def silu_s(p, s):
                    a.wait_ge(r["gu"], s + 1 + 2)
                    a.wait_ge(r["hid"], s + 1)
                    a.activation(gate[:, p, :], CC[:, 512 * p:512 * p + H], ACT.Silu).then_inc(r["silu"], 1)

                def rowsT_s(p, s):
                    a.wait_ge(r["rowsT"], s + 1 + RING)
                    a.wait_ge(r["gu"], s + 1)
                    a.activation(rowsT[:, p, :], (A, B)[p][:, 0:D], ACT.Copy).then_inc(r["rowsT_sb"], 1)

                def y_s(u, s, round_):
                    a.wait_ge(r["y"], s + 1 + 2)
                    a.wait_ge(r[f"st{u % RING}"], 16 * (round_ + 1))
                    a.activation(y_sb[:, u % RING, :], SS[:, 512 * (u % 2):512 * (u % 2) + D], ACT.Copy
                                 ).then_inc(r["y_sb"], 1)

                rowsT_s(0, 0)
                rowsT_s(1, 1)
                silu_s(0, 0)
                NB = (SLOT_TILES - 4) // RING
                with a.Fori(0, NB) as j:
                    for u in range(1, 5):
                        s = RING * j + u
                        rowsT_s((u + 1) % 2, s + 1)
                        silu_s(u % 2, s)
                        y_s(u - 1, s - 1, j)
                for s in range(RING * NB + 1, SLOT_TILES + 1):
                    if s + 1 < SLOT_TILES:
                        rowsT_s((s + 1) % 2, s + 1)
                    if s < SLOT_TILES:
                        silu_s(s % 2, s)
                    y_s(s - 1, s - 1, (s - 1) // RING)

            def attention():
                t = T

                def turn(i, u):
                    if there(i + 1):
                        b, q = i + 1, (u + 1) % 2
                        a.wait_ge(t["qh"], b + 1)
                        a.activation(qh[:, :], CC[:, 0:512], ACT.Copy, scale=SCALE).then_inc(t["qh_sb"], 1)
                        a.wait_ge(t["vh"], b + 1)
                        a.activation(vo[:, q, :], F[:, :], ACT.Copy).then_inc(t["vo_sb"], 1)
                    if there(i):
                        a.wait_ge(t["prT"], i + 1)
                        a.activation(prT[:, 0:4, :], CC[:, 0:512].rearrange("p (h n) -> p h n", h=4),
                                     ACT.Copy).then_inc(t["prT_a"], 1)
                    if there(i + 3):
                        b, q = i + 3, (u + 3) % 2
                        a.wait_ge(t["xT"], b + 1)
                        if there(i - POST):
                            a.wait_ge(t["hrT"], i - POST + 1)
                        after(a, t["qk"], b - 1)
                        after(a, t["v"], b - 1)
                        after(a, t["halo"], b - 1)
                        a.activation(xT[:, q, :, TAPS - 1:], A[:, 0:D].rearrange("p (c n) -> p c n", c=DC),
                                     ACT.Copy).then_inc(t["xT_sb"], 1)
                    if there(i - POST):
                        b = i - POST
                        a.wait_ge(t["hrT"], b + 1)
                        after(a, t["logits"], b)
                        a.activation(hT_sb[:, 0, :], A[:, D:2 * D], ACT.Copy).then_inc(t["hrT_sb"], 1)
                    if there(i + 1):
                        b, q = i + 1, (u + 1) % 2
                        a.wait_ge(t["max"], b + 1)
                        after(a, t["prT"], b - 1)
                        for h in range(NH):
                            e = a.activation(pr[:, q, h, :], SS[:, h * P:(h + 1) * P], ACT.Exp,
                                             bias=nmax[:, q, h:h + 1], accum_out=psums[:, q, h:h + 1])
                        e.then_inc(t["exp"], 1)

                a.wait_ge(wprep, 1)
                a.activation(vo_sb[:, :], A[0:W + 1, :], ACT.Copy).then_inc(wprep, 1)
                a.preload_act_table(ACT.Exp)
                turns(a, turn)

            def first_copies():
                with a.Fori(0, TILES // 2) as j:
                    for p in range(2):
                        a.wait_ge(first["transposed"], 2 * j + p + 1)
                        a.activation(hT_sb[:, p, :], (A, B)[p][:, 0:D], ACT.Copy).then_inc(first["copied"], 1)

            def difference(r):
                a.wait_ge(r["diff"], 1)
                a.activation(wtmp[:, 0, :], wtmp[:, 1, :], ACT.Exp).then_inc(r["expd"], 1)

            a.sem_inc(first["copied"], 2)
            first_copies()
            end_phase(a, 0)
            difference(R[0])
            end_phase(a, 1)
            experts(R[0])
            end_phase(a, 2)
            attention()
            end_phase(a, 3)
            difference(R[1])
            end_phase(a, 4)
            experts(R[1])
            end_phase(a, 5)

        @block.vector
        def _(v):
            st = Steps(v, dve)
            v.wait_ge(made, N_CONST)
            v.tensor_copy(ident_bf[:, :], ident[:, :]).then_inc(const, 1)
            v.tensor_copy(iota_f[:, :], iota_i[:, :]).then_inc(const, 1)
            v.tensor_copy(iota_bf[:, :], iota_i[:, :]).then_inc(const, 1)
            v.tensor_copy(part_f[:, :], part_i[:, :]).then_inc(const, 1)
            v.wait_ge(const, 4)
            v.tensor_scalar(erank[:, :], iota_f[:, 0:E], -float(E), None, ALU.add).then_inc(const, 1)
            v.wait_ge(const, 5)

            def newton(cols):
                va, g, t = var[:, 0:cols], rstd[:, 0:cols], nt[:, 0:cols]
                st.did(v.tensor_scalar(t.bitcast(I32), va.bitcast(I32), 1, None, ALU.logical_shift_right))
                st.wait()
                st.did(v.tensor_scalar(g.bitcast(I32), t.bitcast(I32), -1.0, RSQRT_SEED, ALU.mult, ALU.add))
                st.wait()
                for _ in range(3):
                    st.did(v.tensor_tensor(t, g, g, ALU.mult))
                    st.wait()
                    st.did(v.scalar_tensor_tensor(out=t, in0=t, scalar=-0.5, in1=va, op0=ALU.mult, op1=ALU.mult))
                    st.wait()
                    st.did(v.scalar_tensor_tensor(out=g, in0=t, scalar=1.5, in1=g, op0=ALU.add, op1=ALU.mult))
                    st.wait()

            def first_norm():
                for g in range(GROUPS):
                    v.wait_ge(x_in[g], 16)
                    for u in range(GROUP):
                        st.did(v.bn_stats(stats[:, u, :], x_tile(GROUP * g + u)))
                    st.wait()
                    v.sem_inc(passed_dve, 1)
                    for u in range(GROUP):
                        st.did(v.bn_aggr(mv[:, u, :], stats[:, u, :]))
                    st.wait()
                    st.did(v.tensor_scalar(var[:, :], mv[:, :, 1], EPS, None, ALU.add))
                    st.wait()
                    newton(GROUP)
                    if g:
                        v.wait_ge(first["stored"], 16 * g)
                    for u in range(GROUP):
                        if g:
                            v.wait_ge(first["transposed"], GROUP * (g - 1) + u + 1)
                        v.tensor_scalar(h_ring[:, u, :], x_tile(GROUP * g + u), mv[:, u, 0:1],
                                        rstd[:, u:u + 1], ALU.subtract, ALU.mult).then_inc(first["normed"], 1)

            def add_experts(z, t, q, rows_in):
                v.wait_ge(z[f"g{q}"], rows_in)
                for k in range(TOPK):
                    st.did(v.scalar_tensor_tensor(out=x_tile(t), in0=yg[:, q, k, :], scalar=wts[:, k, bass.ds(t, 1)],
                                                  in1=x_tile(t), op0=ALU.mult, op1=ALU.add))
                    st.wait()
                v.sem_inc(z["combined"], 1)

            def last_sum():
                v.sem_inc(last["combined"], 2)
                with v.Fori(0, TILES // 2) as j:
                    st.enter(j, 2 * TOPK)
                    for q in range(2):
                        add_experts(last, 2 * j + q, q, 16 * TOPK * (j + 1))
                        v.sem_inc(final, 1)
                st.leave(TILES // 2)

            def route(L, from_psum):
                r = R[L]

                def step(i):
                    st.did(i)
                    st.wait()

                def over_e(ap):
                    return ap.unsqueeze(2).to_broadcast([P, TILES, E])

                if from_psum:
                    step(v.tensor_copy(lg[:, :, :], F[:, 0:TILES * E].rearrange("p (i e) -> p i e", e=E)))
                src = lg
                ranks = erank[:, :].unsqueeze(1).to_broadcast([P, TILES, E])
                for k in range(TOPK):
                    step(v.tensor_reduce(top[:, k, :], src[:, :, :], AX.X, ALU.max))
                    step(v.tensor_tensor(tmp[:, :, :], src[:, :, :], over_e(top[:, k, :]), ALU.is_equal))
                    step(v.tensor_tensor(tmp[:, :, :], tmp[:, :, :], ranks, ALU.mult))
                    step(v.tensor_reduce(pick[:, k, :], tmp[:, :, :], AX.X, ALU.min))
                    step(v.tensor_tensor(oh[:, k, :, :], over_e(pick[:, k, :]), ranks, ALU.is_equal))
                    if k == 0:
                        step(v.scalar_tensor_tensor(out=lg2[:, :, :], in0=oh[:, 0, :, :], scalar=-3.0e38,
                                                    in1=lg[:, :, :], op0=ALU.mult, op1=ALU.add))
                        src = lg2
                v.tensor_tensor(sel_bf[:, :].rearrange("p (i e) -> p i e", e=E), oh[:, 0, :, :], oh[:, 1, :, :],
                                ALU.add).then_inc(r["picked"], 1)
                v.tensor_tensor(wtmp[:, 1, :], top[:, 1, :], top[:, 0, :], ALU.subtract).then_inc(r["diff"], 1)
                v.wait_ge(r["counted"], 1)
                step(v.tensor_copy(tot[:, :, :], B[:, 0:TILES * E].rearrange("p (i e) -> p e i", e=E)))
                step(v.tensor_tensor_scan(cum[:, :, :].rearrange("p e i -> p (e i)"),
                                          tot[:, :, :].rearrange("p e i -> p (e i)"), zeros[:, :], 0.0,
                                          ALU.add, ALU.add))
                ends = cum[:, :, TILES - 1]
                step(v.tensor_copy(ecnt[:, 0:1], cum[:, 0, TILES - 1:TILES]))
                step(v.tensor_tensor(ecnt[:, 1:E], cum[:, 1:E, TILES - 1], cum[:, 0:E - 1, TILES - 1], ALU.subtract))
                step(v.tensor_scalar(etil[:, :], ecnt[:, :], P / 2 - 0.5, 1.0 / P, ALU.add, ALU.mult))
                step(v.tensor_scalar(etil[:, :], etil[:, :], MAGIC, MAGIC, ALU.add, ALU.subtract))
                step(v.tensor_tensor_scan(etcum[:, :], etil[:, :], zeros[:, 0:E], 0.0, ALU.add, ALU.add))
                step(v.tensor_tensor(eadj[:, :], etcum[:, :], etil[:, :], ALU.subtract))
                step(v.scalar_tensor_tensor(out=eadj[:, :], in0=eadj[:, :], scalar=float(P), in1=ecnt[:, :],
                                            op0=ALU.mult, op1=ALU.add))
                step(v.tensor_tensor(eadj[:, :], eadj[:, :], ends, ALU.subtract))
                step(v.tensor_tensor(cum[:, :, :], cum[:, :, :], tot[:, :, :], ALU.subtract))
                step(v.tensor_tensor(cum[:, :, :], cum[:, :, :], eadj[:, :].unsqueeze(2).to_broadcast([P, E, TILES]),
                                     ALU.add))
                step(v.tensor_tensor(lg[:, :, :], A[:, 0:TILES * E].rearrange("p (i e) -> p i e", e=E),
                                     cum[:, :, :].rearrange("p e i -> p i e"), ALU.add))
                for k in range(TOPK):
                    step(v.tensor_tensor(tmp[:, :, :], lg[:, :, :], oh[:, k, :, :], ALU.mult))
                    step(v.tensor_reduce(slot[:, k, :], tmp[:, :, :], AX.X, ALU.add))
                step(v.tensor_copy(slot_i[:, :, :], slot[:, :, :]))
                step(v.tensor_scalar(stile[:, :, :], slot[:, :, :], 0.5 - P / 2, 1.0 / P, ALU.add, ALU.mult))
                step(v.tensor_scalar(stile[:, :, :], stile[:, :, :], MAGIC, MAGIC, ALU.add, ALU.subtract))
                step(v.scalar_tensor_tensor(out=slane[:, :, :], in0=stile[:, :, :], scalar=-float(P),
                                            in1=slot[:, :, :], op0=ALU.mult, op1=ALU.add))
                step(v.tensor_tensor(eidw[:, :, :], etcum[0:1, :].unsqueeze(1).to_broadcast([1, SLOT_TILES, E]),
                                     iota_f[0:1, 0:SLOT_TILES].unsqueeze(2).to_broadcast([1, SLOT_TILES, E]),
                                     ALU.is_le))
                step(v.tensor_reduce(eidf[:, :], eidw[:, :, 0:E - 1], AX.X, ALU.add))
                step(v.tensor_copy(eid_i[:, :], eidf[:, :]))
                v.wait_ge(r["expd"], 1)
                step(v.tensor_scalar(wtmp[:, 1, :], wtmp[:, 0, :], 1.0, None, ALU.add))
                step(v.reciprocal(wtmp[:, 1, :], wtmp[:, 1, :]))
                step(v.tensor_scalar(wts[:, 0, :], wtmp[:, 1, :], 0.5, None, ALU.mult))
                step(v.tensor_tensor(wts[:, 1, :], wts[:, 0, :], wtmp[:, 0, :], ALU.mult))
                with v.Fori(0, TILES // 2) as j:
                    for p in range(2):
                        i = 2 * j + p
                        v.wait_ge(r["tabled"], i + 1)
                        for k in range(TOPK):
                            col = bass.ds(i, 1)
                            v.tensor_scalar(lane_oh[:, p, k, :], iota_bf[:, :], slane[:, k, col], None, ALU.is_equal)
                            v.tensor_scalar(tile_oh[:, p, k, 0:SLOT_TILES], iota_bf[:, 0:SLOT_TILES],
                                            stile[:, k, col], part_f[:, 0:1], ALU.is_equal, ALU.mult)
                            ins = v.tensor_scalar(tile_oh[:, p, k, SLOT_TILES:], iota_bf[:, 0:SLOT_TILES],
                                                  stile[:, k, col], iota_f[:, col], ALU.is_equal, ALU.mult)
                        ins.then_inc(r["onehot"], 1)
                v.wait_ge(r["table"], 1)
                step(v.tensor_scalar(tokf[:, :], G[:, SLOT_TILES:2 * SLOT_TILES], float(P), None, ALU.mult))
                step(v.tensor_tensor(tokf[:, :], tokf[:, :], G[:, 0:SLOT_TILES], ALU.add))
                step(v.tensor_copy(tok_i[:, :], tokf[:, :]))

            def experts(r):
                v.sem_inc(r["hid"], 2)
                v.sem_inc(r["hidT_sb"], 2)

                def hid_s(p, s):
                    v.wait_ge(r["silu"], s + 1)
                    v.wait_ge(r["hidT"], s + 1)
                    v.tensor_tensor(hid[:, p, :], gate[:, p, :], CC[:, 512 * p + H:512 * p + GU], ALU.mult
                                    ).then_inc(r["hid"], 1)

                def hidT_s(p, s):
                    v.wait_ge(r["hidT"], s + 1 + 2)
                    v.wait_ge(r["y"], s + 1)
                    v.tensor_copy(hidT[:, p, 0:P], (F, G)[p][:, 0:P])
                    v.tensor_copy(hidT[0:H - P, p, P:2 * P], (F, G)[p][0:H - P, P:2 * P]).then_inc(r["hidT_sb"], 1)

                hid_s(0, 0)
                NB = (SLOT_TILES - 4) // RING
                with v.Fori(0, NB) as j:
                    for u in range(1, 5):
                        s = RING * j + u
                        hidT_s((u - 1) % 2, s - 1)
                        hid_s(u % 2, s)
                for s in range(RING * NB + 1, SLOT_TILES + 1):
                    hidT_s((s - 1) % 2, s - 1)
                    if s < SLOT_TILES:
                        hid_s(s % 2, s)

            def attention():
                t = T

                def stats_of(b, col):
                    st.did(v.bn_stats(stats[:, col, :], x_tile(b)))
                    st.wait()
                    v.sem_inc(passed_dve, 1)
                    st.did(v.bn_aggr(mv4[:, col, :], stats[:, col, :]))

                def turn(i, u):
                    if there(i):
                        v.wait_ge(t["exp"], i + 1)
                        v.reciprocal(prec[:, u, :], psums[:, u, :]).then_inc(t["rec"], 1)
                    if there(i + 2):
                        b, q = i + 2, u
                        v.wait_ge(t["xT_sb"], b + 1)
                        after(v, t["qk"], b)
                        after(v, t["v"], b)
                        v.tensor_scalar(xT[:, 1 - q, :, 0:TAPS - 1], xT[:, q, :, P:P + TAPS - 1],
                                        keep[:, bass.ds(b, 1)], None, ALU.mult).then_inc(t["halo"], 1)
                    if there(i + 1):
                        v.wait_ge(t["kh"], i + 2)
                        v.tensor_copy(kh[:, :], CC[:, 512:1024]).then_inc(t["kh_sb"], 1)
                    if u == 0 and (there(i + 4) or there(i - POST) or there(i - POST + 1)):
                        st.wait()
                        st.did(v.tensor_scalar(var[:, 0:4], mv4[:, :, 1], EPS, None, ALU.add))
                        st.wait()
                        newton(4)
                        for b, dst, done, col in ((i + 3, ha, t["normed"], 0), (i - POST, hr, t["routed"], 2)):
                            for k in range(2):
                                if not there(b + k):
                                    continue
                                if col == 0:
                                    after(v, t["xT"], b + k - 1)
                                    place = 1 - k
                                else:
                                    after(v, t["hrT"], b + k - 1)
                                    after(v, t[f"stored{k}"], 8 * (b - 1 if k == 0 else b + 1))
                                    place = k
                                v.tensor_scalar(dst[:, place, :], x_tile(b + k), mv4[:, col + k, 0:1],
                                                rstd[:, col + k:col + k + 1], ALU.subtract, ALU.mult
                                                ).then_inc(done, 1)
                    if there(i + 1):
                        q = (u + 1) % 2
                        v.wait_ge(t["scores"], i + 2)
                        st.did(v.tensor_reduce(nmax[:, q, :], SS[:, :].rearrange("p (h s) -> p h s", s=P), AX.X,
                                               ALU.max))
                        st.wait()
                        v.tensor_scalar(nmax[:, q, :], nmax[:, q, :], -1.0, None, ALU.mult).then_inc(t["max"], 1)
                    if there(i):
                        v.wait_ge(t["prT"], i + 1)
                        v.tensor_copy(prT[:, 4:8, :], CC[:, 512:1024].rearrange("p (h n) -> p h n", h=4)
                                      ).then_inc(t["prT_d"], 1)
                    if there(i - 1):
                        v.wait_ge(t["mhaT"], i)
                        v.tensor_scalar(mhaT[0:W, :], G[0:W, 0:P], bo_sb[:, 0:1], None, ALU.add
                                        ).then_inc(t["mhaT_sb"], 1)
                    if there(i + PRE):
                        b, q = i + PRE, (u + PRE) % 2
                        add_experts(t, b, q, 8 * TOPK * (b - q + 2))
                        stats_of(b, u)
                    if there(i + 2):
                        v.wait_ge(t["v"], i + 3)
                        v.tensor_scalar(qT[0:W, :], B[0:W, 0:P], convb_sb[0:W, 0:1], None, ALU.add)
                        v.tensor_scalar(kT[0:W, :], B[W:2 * W, 0:P], convb_sb[W:2 * W, 0:1], None, ALU.add)
                        v.tensor_scalar(vT[0:W, :], B[0:W, P:2 * P], convb_sb[0:W, 1:2], None, ALU.add
                                        ).then_inc(t["qkv_sb"], 1)
                    if there(i - 1):
                        b = i - 1
                        v.wait_ge(t["out"], b + 1)
                        st.did(v.tensor_tensor(x_tile(b), x_tile(b), G[:, D:2 * D], ALU.add))
                        st.wait()
                        v.sem_inc(t["res"], 1)
                        stats_of(b, 2 + u)
                    if there(i - POST):
                        b = i - POST
                        v.wait_ge(t["logits"], b + 1)
                        v.tensor_copy(lg[:, bass.ds(b, 1), :].rearrange("p a e -> p (a e)"), G[:, P:P + E]
                                      ).then_inc(t["lg"], 1)
                    if there(i):
                        v.wait_ge(t["mha"], i + 1)
                        v.tensor_copy(mha[:, :], F[:, 0:W]).then_inc(t["mha_sb"], 1)

                st.did(v.memset(mv4[:, :, :], 1.0))
                v.memset(xT[:, 0, :, 0:TAPS - 1], 0.0).then_inc(const, 1)
                turns(v, turn, st, 12 + 2 * (1 + TOPK + 2 + 3))

            first_norm()
            end_phase(v, 0)
            v.wait_ge(loaded, 16 * len(loads))
            route(0, True)
            end_phase(v, 1)
            experts(R[0])
            end_phase(v, 2)
            attention()
            end_phase(v, 3)
            route(1, False)
            end_phase(v, 4)
            experts(R[1])
            end_phase(v, 5)
            last_sum()

        @block.tensor
        def _(pe):
            def weights_vo():
                for h in range(NH):
                    i = pe.matmul(A[0:W + 1, h * W:(h + 1) * W], wvT_sb[:, h, :], wo_sb[:, h, :], start=True, stop=True)
                i.then_inc(wprep, 1)
                pe.wait_ge(wprep, 2)

            def first_router():
                z = first

                def turn(u, t):
                    pe.wait_ge(z["normed"], t + 1)
                    pe.wait_ge(z["copied"], t + 1)
                    for c in range(DC):
                        i = pe.transpose((A, B)[u % 2][:, c * P:(c + 1) * P], h_ring[:, u, c * P:(c + 1) * P],
                                         ident[:, :])
                    i.then_inc(z["transposed"], 1)

                def logits(p, t):
                    pe.wait_ge(z["copied"], t + 3)
                    for c in range(DC):
                        pe.matmul(F[:, bass.ds(t * E, E)], hT_sb[:, p, c * P:(c + 1) * P], rw_sb[:, c * E:(c + 1) * E],
                                  start=(c == 0), stop=(c == DC - 1))

                turn(0, 0)
                for u in range(1, GROUP):
                    turn(u, u)
                    logits(1 - u % 2, u - 1)
                with pe.Fori(1, GROUPS) as g:
                    for u in range(GROUP):
                        turn(u, GROUP * g + u)
                        logits(1 - u % 2, GROUP * g + u - 1)
                logits(1, TILES - 1)

            def route(L):
                r = R[L]
                pe.wait_ge(r["picked"], 1)
                pe.matmul(A[:, 0:TILES * E], before_bf[:, :], sel_bf[:, :], start=True, stop=True)
                pe.matmul(B[:, 0:TILES * E], ones_bf[:, :], sel_bf[:, :], start=True, stop=True).then_inc(r["counted"], 1)
                n = 2 * SLOT_TILES
                pe.matmul(G[:, 0:n], zeros_bf[:, 0:P], zeros_bf[:, 0:n], start=True, stop=False,
                          skip_group_check=True)
                pe.sem_inc(r["tabled"], 2)
                with pe.Fori(0, TILES // 2) as j:
                    for p in range(2):
                        pe.wait_ge(r["onehot"], 2 * j + p + 1)
                        for k in range(TOPK):
                            i = pe.matmul(G[:, 0:n], lane_oh[:, p, k, :], tile_oh[:, p, k, :], start=False,
                                          stop=False, skip_group_check=True)
                        i.then_inc(r["tabled"], 1)
                pe.matmul(G[:, 0:n], zeros_bf[:, 0:P], zeros_bf[:, 0:n], start=False, stop=True,
                          skip_group_check=True).then_inc(r["table"], 1)

            def experts(r):
                pe.sem_inc(r["rowsT"], RING)
                pe.sem_inc(r["gu"], 2)
                pe.sem_inc(r["hidT"], 2)
                pe.sem_inc(r["y"], 2)

                def expert_of(s):
                    return pe.value_load(eid_i[0:1, bass.ds(s, 1)], min_val=0, max_val=E - 1)

                def turn_rows(u, s, grp):
                    pe.wait_ge(r[f"g{u % RING}"], 16 * (grp + 1))
                    pe.wait_ge(r["rowsT_sb"], s + 1)
                    for c in range(DC):
                        i = pe.transpose((A, B)[u % 2][:, c * P:(c + 1) * P], rows[:, u % RING, c * P:(c + 1) * P],
                                         ident[:, :])
                    i.then_inc(r["rowsT"], 1)

                def gate_up(u, s, e):
                    pe.wait_ge(r["rowsT_sb"], s + 1 + 2)
                    pe.wait_ge(r["hid"], s + 1)
                    for c in range(DC):
                        i = pe.matmul(CC[:, 512 * (u % 2):512 * (u % 2) + GU], rowsT[:, u % 2, c * P:(c + 1) * P],
                                      gup_sb[:, bass.ds(e * (DC * GU) + c * GU, GU)], start=(c == 0), stop=(c == DC - 1))
                    i.then_inc(r["gu"], 1)

                def turn_hid(u, s):
                    pe.wait_ge(r["hid"], s + 1 + 2)
                    pe.wait_ge(r["hidT_sb"], s + 1)
                    for c, (o, w) in enumerate(HC):
                        i = pe.transpose((F, G)[u % 2][0:w, c * P:(c + 1) * P], hid[:, u % 2, o:o + w], ident[:, :])
                    i.then_inc(r["hidT"], 1)

                def down(u, s, e):
                    pe.wait_ge(r["hidT_sb"], s + 1 + 2)
                    pe.wait_ge(r["y_sb"], s + 1)
                    for c, (o, w) in enumerate(HC):
                        i = pe.matmul(SS[:, 512 * (u % 2):512 * (u % 2) + D], hidT[0:w, u % 2, c * P:(c + 1) * P],
                                      dp_sb[0:w, bass.ds(e * (2 * D) + c * D, D)], start=(c == 0), stop=(c == 1))
                    i.then_inc(r["y"], 1)

                def step(u, s, grp_next, last_e):
                    if grp_next is not None:
                        turn_rows(u + 1, s + 1, grp_next)
                    turn_hid(u - 1, s - 1)
                    e = None
                    if not isinstance(s, int) or s < SLOT_TILES:
                        e = expert_of(s)
                        gate_up(u, s, e)
                    down(u - 1, s - 1, last_e)
                    return e

                turn_rows(0, 0, 0)
                turn_rows(1, 1, 0)
                gate_up(0, 0, expert_of(0))
                NB = (SLOT_TILES - 4) // RING
                with pe.Fori(0, NB) as j:
                    e = expert_of(RING * j)
                    for u in range(1, 5):
                        e = step(u, RING * j + u, j + (u + 1) // RING, e)
                e = expert_of(RING * NB)
                for s in range(RING * NB + 1, SLOT_TILES + 1):
                    e = step(s, s, (s + 1) // RING if s + 1 < SLOT_TILES else None, e)

            def attention():
                t = T

                def turn(i, u):
                    if there(i + 1):
                        b, q = i + 1, (u + 1) % 2
                        pe.wait_ge(t["qkv_sb"], b + 1)
                        after(pe, t["prT_a"], i)
                        after(pe, t["prT_d"], i)
                        for o, wgt, src, done in ((0, wq_sb, qT, "qh"), (512, wk_sb, kT, "kh")):
                            for m in range(4):
                                x = pe.matmul(CC[:, o + m * P:o + (m + 1) * P], wgt[:, m * P:(m + 1) * P], src[:, :],
                                              start=True, stop=True)
                            x.then_inc(t[done], 1)
                        after(pe, t["mha_sb"], i)
                        after(pe, t["vo_sb"], b)
                        pe.matmul(F[:, :], vT[:, :], vo_sb[:, :], start=True, stop=True).then_inc(t["vh"], 1)
                        pe.wait_ge(t["qh_sb"], b + 1)
                        pe.wait_ge(t["kh_sb"], b + 1)
                        after(pe, t["exp"], b)
                        for m in range(2):
                            pe.matmul(SS[:, 512 * m:512 * (m + 1)], ident_bf[:, :], mask_bf[:, :], start=True,
                                      stop=False, skip_group_check=True)
                        for h in range(NH):
                            lo, at, m = KD * (h % 2), HEAD_AT[h], h // 2
                            x = pe.matmul(SS[:, at * P:(at + 1) * P], qh[lo:lo + KD, m * P:(m + 1) * P],
                                          kh[lo:lo + KD, m * P:(m + 1) * P], start=False, stop=(m == 3),
                                          skip_group_check=True)
                        x.then_inc(t["scores"], 1)
                    if there(i - 1):
                        pe.wait_ge(t["mha_sb"], i)
                        after(pe, t["res"], i - 1)
                        after(pe, t["lg"], i - POST)
                        pe.sem_inc(passed_pe, 1)
                        pe.transpose(G[0:W, 0:P], mha[:, :], ident[:, :]).then_inc(t["mhaT"], 1)
                    if there(i):
                        pe.wait_ge(t["norm"], i + 1)
                        for h in range(NH):
                            x = pe.transpose(CC[:, h * P:(h + 1) * P], pr[:, u, h, :], ident[:, :])
                        x.then_inc(t["prT"], 1)
                    if there(i + 3):
                        b, q = i + 3, (u + 1) % 2
                        pe.wait_ge(t["normed"], b + 1)
                        after(pe, t["xT_sb"], b)
                        after(pe, t["hrT_sb"], i - POST)
                        for c in range(DC):
                            x = pe.transpose(A[:, c * P:(c + 1) * P], ha[:, q, c * P:(c + 1) * P], ident[:, :])
                        x.then_inc(t["xT"], 1)
                    if there(i - POST):
                        b, q = i - POST, (u + POST) % 2
                        pe.wait_ge(t["routed"], b + 1)
                        after(pe, t["hrT_sb"], b)
                        if not there(i + 3):
                            pe.wait_ge(t["xT_sb"], TILES)
                        for c in range(DC):
                            x = pe.transpose(A[:, D + c * P:D + (c + 1) * P], hr[:, u, c * P:(c + 1) * P],
                                             ident[:, :])
                        x.then_inc(t["hrT"], 1)
                    if there(i + 2):
                        b, q = i + 2, u
                        pe.wait_ge(t["xT_sb"], b + 1)
                        after(pe, t["halo"], b)
                        after(pe, t["qkv_sb"], b)
                        for o, w, dst, done in ((0, 2 * W, B[:, 0:P], "qk"), (2 * W, W, B[0:W, P:2 * P], "v")):
                            for c in range(DC):
                                for k in range(TAPS):
                                    x = pe.matmul(dst, conv_sb[:, k * DC + c, o:o + w], xT[:, q, c, k:k + P],
                                                  start=(c == 0 and k == 0), stop=(c == DC - 1 and k == TAPS - 1))
                            x.then_inc(t[done], 1)
                    if there(i - 1):
                        pe.wait_ge(t["mhaT_sb"], i)
                    if there(i - POST):
                        if not there(i - 1):
                            pe.wait_ge(t["res"], TILES)
                        pe.wait_ge(t["hrT_sb"], i - POST + 1)
                        after(pe, t["lg"], i - POST)
                        for c in range(DC):
                            x = pe.matmul(G[:, P:P + E], hT_sb[:, 0, c * P:(c + 1) * P], rw_sb[:, c * E:(c + 1) * E],
                                          start=(c == 0), stop=(c == DC - 1))
                        x.then_inc(t["logits"], 1)
                    if there(i - 1):
                        pe.matmul(G[:, D:2 * D], mhaT[:, :], proj_sb[:, :], start=True, stop=True
                                  ).then_inc(t["out"], 1)
                    if there(i):
                        pe.wait_ge(t["prT_a"], i + 1)
                        pe.wait_ge(t["prT_d"], i + 1)
                        pe.wait_ge(t["vo_sb"], i + 2 if there(i + 1) else i + 1)
                        for h in range(NH):
                            x = pe.matmul(F[:, 0:W], prT[:, HEAD_AT[h], :], vo[:, u, h * W:(h + 1) * W],
                                          start=(h == 0), stop=(h == NH - 1))
                        x.then_inc(t["mha"], 1)

                turns(pe, turn)

            pe.wait_ge(rw_in, 16)
            pe.wait_ge(const, 5)
            first_router()
            pe.wait_ge(loaded, 16 * len(loads))
            end_phase(pe, 0)
            route(0)
            end_phase(pe, 1)
            experts(R[0])
            end_phase(pe, 2)
            weights_vo()
            pe.wait_ge(const, 6)
            attention()
            end_phase(pe, 3)
            route(1)
            end_phase(pe, 4)
            experts(R[1])
            end_phase(pe, 5)


def kernel(**inputs):
    import numpy as _np
    import concourse.bacc as _bacc
    from concourse import mybir as _mybir
    from concourse.bass_utils import run_bass_kernel_spmd as _run

    a = {n: _np.asarray(v) for n, v in inputs.items()}
    f32 = {
        "x": a["L0_attn_x"],
        "conv_w": a["L0_attn_conv_w"].reshape(TAPS, DC, P, 3 * W).transpose(2, 0, 1, 3).reshape(P, TAPS * DC, 3 * W),
        "conv_b": a["L0_attn_conv_b"].reshape(3 * W, 1),
        "wq": a["L0_attn_wq"].reshape(W, NH * KD),
        "wk": a["L0_attn_wk"].reshape(W, NH * KD),
        "wvT": _np.concatenate([a["L0_attn_wv"].transpose(2, 1, 0), a["L0_attn_bv"].T.reshape(KD, NH, 1)], 2),
        "wo": a["L0_attn_wo"].transpose(1, 0, 2),
        "bq": a["L0_attn_bq"].reshape(1, NH * KD),
        "bk": a["L0_attn_bk"].reshape(1, NH * KD),
        "bo": a["L0_attn_bo"].reshape(W, 1),
        "proj_w": a["L0_attn_proj_w"],
        "proj_b": a["L0_attn_proj_b"].reshape(1, D),
        "gupT": a["L0_ffn_gate_up_proj"].reshape(E, GU, DC, P).transpose(3, 0, 2, 1).reshape(P, E * DC * GU),
        "dpT": a["L0_ffn_down_proj"].transpose(2, 0, 1),
        "rwT": a["L0_ffn_router_w"].reshape(E, DC, P).transpose(2, 1, 0).reshape(P, DC * E),
    }
    nc = _bacc.Bacc("TRN2", target_bir_lowering=False, num_devices=1)
    arrays, args = {}, []
    for name, v in f32.items():
        v = _np.ascontiguousarray(v)
        arrays[f"in_{name}_dram"] = v
        args.append(nc.dram_tensor(f"in_{name}_dram", v.shape, _mybir.dt.from_np(v.dtype), kind="ExternalInput").ap())
    args.append(nc.dram_tensor("out_0_dram", (BATCH, SEQ, D), F32, kind="ExternalOutput").ap())
    args.append(nc.dram_tensor("h_rows", (TOKENS, D), F32, kind="Internal").ap())
    args.append(nc.dram_tensor("y_rows", (SLOT_TILES * P, D), F32, kind="Internal").ap())
    macaron_kernel(nc, *args)
    r = _run(nc, [arrays], core_ids=[0])
    return r.results[0]["out_0_dram"]
```

```python
from contextlib import ExitStack

import numpy as np

import concourse.bass as bass
from concourse import mybir

ALU = mybir.AluOpType
ACT = mybir.ActivationFunctionType
AX = mybir.AxisListType
F32 = mybir.dt.float32
F32R = mybir.dt.float32r
BF16 = mybir.dt.bfloat16
I32 = mybir.dt.int32

P = 128
BATCH, SEQ, D = 2, 2048, 256
TOKENS = BATCH * SEQ
TILES = TOKENS // P
DC = D // P
E, TOPK = 8, 2
H = 176
GU = 2 * H
HW = H // 2
HC = ((0, HW), (HW, HW))
EW = DC * GU + 2 * D
SLOT_TILES = (TOPK * TOKENS + E * (P - 1)) // P
SLOT_TILES += SLOT_TILES % 2
TAPS, W = 3, 64
NH, KD = 8, 64
SCALE = float(KD) ** -0.5
LG_AT = 3 * P
V_AT = TAPS * 2 * W
HEAD_AT = [4 * (h % 2) + h // 2 for h in range(NH)]
PRE, POST = 6, 4
GROUP = 8
GROUPS = TILES // GROUP
BATCHED = 4
EPS = 1e-5
MAGIC = 12582912.0
RSQRT_SEED = float(0x5F3759DF)
MASKED = -1e9


class Overlay:

    def __init__(self, tensor):
        self.tensor, self.at = tensor, 0

    def take(self, rows, n, width):
        first, self.at = self.at, self.at + n * width
        return self.tensor[0:rows, first:self.at].rearrange("p (n w) -> p n w", w=width)


class Steps:

    def __init__(self, eng, sem, gate=None):
        self.eng, self.sem, self.gate, self.n, self.loop = eng, sem, gate, 0, 0

    def did(self, instruction):
        instruction.then_inc(self.sem, 1)
        self.n += 1

    def wait(self):
        self.eng.wait_ge(self.sem, self.loop + self.n)
        if self.gate:
            self.eng.sem_inc(self.gate, 1)

    def enter(self, var, per_round):
        self.n0, self.per_round = self.n, per_round
        self.loop = var * per_round

    def leave(self, rounds):
        assert self.n == self.n0 + self.per_round, (self.n - self.n0, self.per_round)
        self.n, self.loop = self.n0 + rounds * self.per_round, 0


NEWTON = 1 + 3 * 4


def newton(eng, st, va, g, t):
    st.did(eng.tensor_scalar(g.bitcast(I32), va.bitcast(I32), -0.5, RSQRT_SEED, ALU.mult, ALU.add))
    st.wait()
    for _ in range(3):
        st.did(eng.tensor_tensor(t, g, g, ALU.mult))
        st.wait()
        st.did(eng.tensor_tensor(t, t, va, ALU.mult))
        st.wait()
        st.did(eng.tensor_scalar(t, t, -0.5, 1.5, ALU.mult, ALU.add))
        st.wait()
        st.did(eng.tensor_tensor(g, g, t, ALU.mult))
        st.wait()


def macaron_kernel(nc, x, conv_w, conv_b, wq, wk, wvT, wo, bq, bk, bo, proj_w, proj_b, gupT, dpT, rwT,
                   out, h_dram, y_dram):
    ctx = ExitStack()
    with ctx:
        def sb(name, shape, dt=F32):
            return ctx.enter_context(nc.sbuf_tensor(name, shape, dt))

        def pb(name, banks):
            return ctx.enter_context(nc.psum_tensor(name, [P, 512 * banks], F32))

        def sem(name):
            return ctx.enter_context(nc.semaphore(name))

        x_sb = sb("x_sb", [P, TILES * D])
        h_ring = sb("h_ring", [P, GROUP, D])
        w_lo = sb("w_lo", [P, E * EW])
        w_hi = sb("w_hi", [P, E * EW], F32R)
        rw_sb = sb("rw_sb", [P, DC * E])
        conv_sb = sb("conv_sb", [P, DC, TAPS * 3 * W])
        convb_sb = sb("convb_sb", [P, 2])
        wqk_sb = sb("wqk_sb", [W + 1, 2, NH * KD])
        wvT_sb = sb("wvT_sb", [KD, NH, W + 1])
        wo_sb = sb("wo_sb", [KD, NH, W])
        wvo_hi = sb("wvo_hi", [W + 1, NH * W], F32R)
        wvo_lo = sb("wvo_lo", [W + 1, NH * W], F32R)
        bo_sb = sb("bo_sb", [W, 1])
        proj_sb = sb("proj_sb", [W + 1, D])
        ident = sb("ident", [P, P])
        before_bf = sb("before_bf", [P, P], BF16)
        ones_bf = sb("ones_bf", [P, P], BF16)
        mask = sb("mask", [P, P])
        iota_i = sb("iota_i", [P, P], I32)
        iota_f = sb("iota_f", [P, P])
        part_i = sb("part_i", [P, 1], I32)
        part_f = sb("part_f", [P, 1])
        erank = sb("erank", [P, E])
        zeros = sb("zeros", [P, TILES * E])
        keep = sb("keep", [P, TILES])
        stats = sb("stats", [P, GROUP, 6])
        mv = sb("mv", [P, GROUP, 2])
        var = sb("var", [P, GROUP])
        rstd = sb("rstd", [P, GROUP])
        nt = sb("nt", [P, GROUP])
        shared = sb("shared", [P, 3584])
        hT_sb = sb("hT_sb", [P, 2, D])
        lg = sb("lg", [P, TILES, E])
        in_routing = Overlay(shared)
        lg2 = in_routing.take(P, TILES, E)
        tmp = in_routing.take(P, TILES, E)
        top = sb("top", [P, TOPK, TILES])
        pick = sb("pick", [P, TOPK, TILES])
        oh = sb("oh", [P, TOPK, TILES, E])
        sel_bf = sb("sel_bf", [P, TILES * E], BF16)
        wts = sb("wts", [P, TOPK, TILES])
        wtmp = sb("wtmp", [P, 2, TILES])
        tot = in_routing.take(P, E, TILES)
        cum = in_routing.take(P, E, TILES)
        ecnt = sb("ecnt", [P, E])
        etil = sb("etil", [P, E])
        etcum = sb("etcum", [P, E])
        eadj = sb("eadj", [P, E])
        slot = sb("slot", [P, TOPK, TILES])
        stile = sb("stile", [P, TOPK, TILES])
        slane = sb("slane", [P, TOPK, TILES])
        slot_i = sb("slot_i", [P, TILES, TOPK], I32)
        eidw = in_routing.take(1, SLOT_TILES, E)
        eidf = sb("eidf", [1, SLOT_TILES])
        at_i = sb("at_i", [1, SLOT_TILES + 2], I32)
        pr = sb("pr", [P, 2, NH, P])
        number = sb("number", [P, TILES])
        h_rings = h_ring[:, :, :], pr[:, :, :, :].rearrange("p b h s -> p (b h s)").rearrange("p (i d) -> p i d", d=D)
        lane_oh = sb("lane_oh", [P, 2, TOPK, BATCHED, P], F32R)
        tile_oh = sb("tile_oh", [P, 2, TOPK, BATCHED, SLOT_TILES], F32R)
        tok_i = sb("tok_i", [P, SLOT_TILES], I32)
        RING = 4
        PAIRS = 4
        stage = sb("stage", [P, 2, RING], I32)
        in_experts = Overlay(shared)
        rows = in_experts.take(P, RING, D)
        rowsT_hi = sb("rowsT_hi", [P, 2, D], F32R)
        rowsT_lo = sb("rowsT_lo", [P, 2, D], F32R)
        gate = in_experts.take(P, 2, H)
        hid = in_experts.take(P, 2, H)
        hidT_hi = sb("hidT_hi", [HW, 2, 2 * P], F32R)
        hidT_lo = sb("hidT_lo", [HW, 2, 2 * P], F32R)
        y_sb = in_experts.take(P, RING, D)
        cstage = sb("cstage", [P, 2, PAIRS * TOPK], I32)
        yg = sb("yg", [P, PAIRS, TOPK, D])
        in_attention = Overlay(shared)
        qh = in_attention.take(P, 1, 512)[:, 0, :]
        kh = in_attention.take(P, 1, 512)[:, 0, :]
        vo = in_attention.take(P, 2, 512)
        prT = in_attention.take(P, NH, P)
        ha = in_attention.take(P, 2, D)
        xT = sb("xT", [P, 2, DC, P + TAPS - 1])
        qk = sb("qk", [W + 1, 2, P])
        vtap = sb("vtap", [W, P])
        vT = sb("vT", [W, P])
        vT_hi = sb("vT_hi", [W + 1, P], F32R)
        vT_lo = sb("vT_lo", [W + 1, P], F32R)
        nmax = sb("nmax", [P, 2, NH])
        psums = sb("psums", [P, 2, NH])
        prec = sb("prec", [P, 2, NH])
        mhaT = sb("mhaT", [W + 1, P])
        hr = sb("hr", [P, 2, D])
        mv4 = sb("mv4", [P, 4, 2])
        var4 = sb("var4", [P, 4])
        nt4 = sb("nt4", [P, 4])
        rstd4 = sb("rstd4", [P, 4])
        minus4 = sb("minus4", [P, 4])
        shift4 = sb("shift4", [P, 4])

        A = pb("A", 1)
        B = pb("B", 1)
        CC = pb("CC", 2)
        F = pb("F", 1)
        SS = pb("SS", 2)
        G = pb("G", 1)

        loaded = sem("loaded")
        made = sem("made")
        const = sem("const")
        phase = sem("phase")
        dve = sem("dve")
        pool_steps = sem("pool_steps")
        wprep = sem("wprep")
        high = sem("high")
        low = sem("low")
        first = {n: sem(f"first_{n}") for n in "normed transposed copied stored0 stored1".split()}
        last = {n: sem(f"last_{n}") for n in "g0 g1 g2 g3 combined gate".split()}
        x_in = [sem(f"x_in{g}") for g in range(GROUPS)]
        R = [dict() for _ in range(2)]
        for L in range(2):
            for n in ("picked", "diff", "expd", "counted", "tiles", "lanes", "numbered", "tabled", "table",
                      "gate_pool", "staged", "g0", "g1", "g2", "g3", "rowsT", "rowsT_hi", "rowsT_lo", "gu", "silu",
                      "hid", "hidT", "hidT_hi", "hidT_lo",
                      "y", "y_sb", "st0", "st1", "st2", "st3"):
                R[L][n] = sem(f"r{L}_{n}")
        T = {n: sem(f"a_{n}") for n in (
            "g0", "g1", "gate", "stage", "combined", "moments", "taken", "rstd", "normed", "xT", "hrT", "xT_sb",
            "hrT_sb", "halo", "conv", "qkv", "qh", "kh", "vh", "qh_sb", "kh_sb", "vo",
            "scores", "max", "exp", "rec", "norm", "prT", "prT_even", "prT_odd", "mha", "mhaT", "out", "logits", "res",
            "lg", "routed", "stored0", "stored1")}
        written = sem("written")
        rw_in = sem("rw_in")
        final = sem("final")
        passed_dve = sem("passed_dve")
        passed_pool = sem("passed_pool")
        ENGINES = 5

        block = ctx.enter_context(nc.Block())
        x_rows = x.rearrange("b s d -> (b s) d").rearrange("(i p) d -> p i d", p=P)
        out_rows = out.rearrange("b s d -> (b s) d").rearrange("(i p) d -> p i d", p=P)
        x_view = x_sb[:, :].rearrange("p (i d) -> p i d", d=D)
        w_view = w_lo[:, :].rearrange("p (e n) -> p e n", n=EW)
        loads = [(w_view[:, :, 0:DC * GU], gupT)]
        loads += [(w_view[0:HW, :, DC * GU + c * D:DC * GU + (c + 1) * D], dpT[o:o + w, :, :])
                  for c, (o, w) in enumerate(HC)]
        loads += [(conv_sb[:, :, :], conv_w), (convb_sb[:, 0:1], conv_b[0:2 * W, :]),
                  (convb_sb[W:2 * W, 1:2], conv_b[2 * W:3 * W, :]), (wqk_sb[0:W, 0, :], wq), (wqk_sb[W:W + 1, 0, :], bq),
                  (wqk_sb[0:W, 1, :], wk), (wqk_sb[W:W + 1, 1, :], bk), (wvT_sb[:, :, :], wvT),
                  (wo_sb[:, :, :], wo), (bo_sb[:, :], bo), (proj_sb[0:W, :], proj_w), (proj_sb[W:W + 1, :], proj_b)]
        N_CONST = 10 + BATCH + 4

        def weight_parts(e):
            for rows_of, at, width in ((P, 0, DC * GU), (HW, DC * GU, 2 * D)):
                cols = bass.ds(e * EW + at, width)
                yield w_lo[0:rows_of, cols], w_hi[0:rows_of, cols], w_lo[0:rows_of, cols].bitcast(F32R)

        def x_tile(t):
            return x_sb[:, bass.ds(t * D, D)]

        def after(eng, sem, n):
            if not isinstance(n, int) or n > 0:
                eng.wait_ge(sem, n)

        FIRST_TURN, LOOP_FROM, LOOP_TO, LAST_TURN = -PRE - 1, 6, TILES - PRE - 2, TILES + POST

        def turns(eng, turn, chain=None, per=0):
            for i in range(FIRST_TURN, LOOP_FROM):
                turn(i, i % 2)
            with eng.Fori(0, (LOOP_TO - LOOP_FROM) // 2) as j:
                if chain:
                    chain.enter(j, per)
                for u in range(2):
                    turn(LOOP_FROM + 2 * j + u, u)
            if chain:
                chain.leave((LOOP_TO - LOOP_FROM) // 2)
            for i in range(LOOP_TO, LAST_TURN):
                turn(i, i % 2)

        ROUNDS = (SLOT_TILES - 4) // RING

        def expert_steps(eng, step):
            for s in range(2):
                step(s, s, 0)
            with eng.Fori(0, ROUNDS) as j:
                for u in range(2, 2 + RING):
                    step(u, RING * j + u, j)
            for s in range(RING * ROUNDS + 2, SLOT_TILES + 2):
                step(s, s, 0)

        def is_tile(s):
            return not isinstance(s, int) or 0 <= s < SLOT_TILES

        def there(b):
            return not isinstance(b, int) or 0 <= b < TILES

        def upto(n):
            return min(n, TILES) if isinstance(n, int) else n

        def end_phase(eng, k):
            eng.drain().then_inc(phase, 1)
            eng.wait_ge(phase, ENGINES * (k + 1))

        @block.sync
        def _(sp):
            for g in range(GROUPS):
                sp.dma_start(x_view[:, g * GROUP:(g + 1) * GROUP, :], x_rows[:, g * GROUP:(g + 1) * GROUP, :]
                             ).then_inc(x_in[g], 16)
                if g == 0:
                    sp.dma_start(rw_sb[:, :], rwT).then_inc(rw_in, 16)
            for dst, src in loads:
                sp.dma_start(dst, src).then_inc(loaded, 16)

            def store_first():
                with sp.Fori(0, GROUPS // 2) as j:
                    for k in range(2):
                        sp.wait_ge(first["normed"], GROUP * (2 * j + k + 1))
                        sp.dma_start(h_dram[bass.ds((2 * j + k) * GROUP * P, GROUP * P), :]
                                     .rearrange("(i p) d -> p i d", p=P), h_rings[k]).then_inc(first[f"stored{k}"], 16)
                for k in range(2):
                    sp.wait_ge(first[f"stored{k}"], 16 * GROUPS // 2)

            def store_second():
                with sp.Fori(0, TILES // 2) as j:
                    for q in range(2):
                        sp.wait_ge(T["routed"], 2 * j + q + 1)
                        sp.dma_start(h_dram[bass.ds((2 * j + q) * P, P), :], hr[:, q, :]
                                     ).then_inc(T[f"stored{q}"], 16)
                for q in range(2):
                    sp.wait_ge(T[f"stored{q}"], 16 * TILES // 2)

            def store_y(L):
                r = R[L]
                for u in range(RING):
                    sp.sem_inc(r[f"st{u}"], 16)
                with sp.Fori(0, SLOT_TILES // RING) as j:
                    for u in range(RING):
                        sp.wait_ge(r["y_sb"], RING * j + u + 1 + 2)
                        sp.dma_start(y_dram[bass.ds((RING * j + u) * P, P), :], y_sb[:, u, :]
                                     ).then_inc(r[f"st{u}"], 16)
                for u in range(RING):
                    sp.wait_ge(r[f"st{u}"], 16 * (SLOT_TILES // RING + 1))

            store_first()
            end_phase(sp, 0)
            end_phase(sp, 1)
            store_y(0)
            end_phase(sp, 2)
            store_second()
            end_phase(sp, 3)
            end_phase(sp, 4)
            store_y(1)
            end_phase(sp, 5)
            with sp.Fori(0, TILES // 2) as g:
                sp.wait_ge(final, 2 * (g + 1))
                sp.dma_start(out_rows[:, bass.ds(2 * g, 2), :], x_view[:, bass.ds(2 * g, 2), :]).then_inc(written, 16)
            sp.wait_ge(written, 16 * (TILES // 2))

        @block.gpsimd
        def _(pool):
            made_n = [0]

            def const_step(ins):
                ins.then_inc(made, 1)
                made_n[0] += 1
                pool.wait_ge(made, made_n[0])

            const_step(pool.memset(ident[:, :], 0.0))
            const_step(pool.affine_select(out=ident[:, :], in_=ident[:, :], compare_op=ALU.not_equal, fill=1.0,
                                          base=0, pattern=[[-1, P]], channel_multiplier=1))
            const_step(pool.memset(ones_bf[:, :], 1.0))
            const_step(pool.affine_select(out=before_bf[:, :], in_=ones_bf[:, :], compare_op=ALU.is_gt, fill=0.0,
                                          base=0, pattern=[[1, P]], channel_multiplier=-1))
            const_step(pool.memset(mask[:, :], 0.0))
            const_step(pool.affine_select(out=mask[:, :], in_=mask[:, :], compare_op=ALU.is_ge, fill=MASKED,
                                          base=0, pattern=[[-1, P]], channel_multiplier=1))
            const_step(pool.iota(iota_i[:, :], pattern=[[1, P]], base=0, channel_multiplier=0))
            const_step(pool.iota(part_i[:, :], pattern=[[0, 1]], base=0, channel_multiplier=1))
            const_step(pool.memset(zeros[:, :], 0.0))
            const_step(pool.memset(keep[:, :], 1.0))
            for b in range(1, BATCH + 1):
                edge = b * TILES // BATCH - 1
                const_step(pool.memset(keep[:, edge:edge + 1], 0.0))
            const_step(pool.memset(mhaT[W:W + 1, :], 1.0))
            const_step(pool.memset(qk[W:W + 1, :, :], 1.0))
            const_step(pool.tensor_copy(vT_hi[W:W + 1, :], ones_bf[0:1, :]))
            const_step(pool.tensor_copy(vT_lo[W:W + 1, :], zeros[0:1, 0:P]))
            assert made_n[0] == N_CONST

            def low_parts(first, last):
                with pool.Fori(first, last) as e:
                    for n, (whole, hi, lo) in enumerate(weight_parts(e)):
                        pool.wait_ge(high, 2 * e + n + 1)
                        pool.tensor_tensor(lo, whole, hi.bitcast(F32), ALU.subtract).then_inc(low, 1)

            def numbers(L):
                r = R[L]
                with pool.Fori(0, TILES // BATCHED // 2) as j:
                    for p in range(2):
                        pool.wait_ge(r["tiles"], 2 * j + p + 1)
                        for k in range(TOPK):
                            ins = pool.tensor_tensor(
                                tile_oh[:, p, k, :, :], tile_oh[:, p, k, :, :].bitcast(F32),
                                number[:, bass.ds((2 * j + p) * BATCHED, BATCHED)].unsqueeze(2)
                                .to_broadcast([P, BATCHED, SLOT_TILES]), ALU.mult)
                        ins.then_inc(r["numbered"], 1)

            def gather_rows(L):
                r = R[L]
                half = 2 * RING
                with pool.Fori(0, SLOT_TILES // half) as j:
                    for k in range(2):
                        pool.wait_ge(r["rowsT"], (2 * j + k) * RING + 1)
                        ids = tok_i[:, bass.ds((2 * j + k) * RING, RING)]
                        pool.tensor_copy(stage[:, k, :], ids).then_inc(r["staged"], 1)
                        pool.wait_ge(r["staged"], 2 * j + k + 1)
                        for u in range(RING):
                            pool.wait_ge(r["rowsT"], (2 * j + k) * RING + u + 1)
                            pool.sem_inc(r["gate_pool"], 1)
                            pool.indirect_dma_start(
                                out=rows[:, u, :], out_offset=None, in_=h_dram[:, :],
                                in_offset=bass.IndirectOffsetOnAxis(ap=stage[:, k, u:u + 1], axis=0)
                            ).then_inc(r[f"g{u}"], 16)

            def gather_pairs(L, z):
                r = R[L]
                with pool.Fori(0, TILES // PAIRS // 2) as j:
                    for half in range(2):
                        first_tile = (2 * j + half) * PAIRS
                        pool.wait_ge(z["combined"], first_tile + 1)
                        pool.tensor_copy(cstage[:, half, :], slot_i[:, bass.ds(first_tile, PAIRS), :]
                                         .rearrange("p i k -> p (i k)")).then_inc(r["staged"], 1)
                        pool.wait_ge(r["staged"], SLOT_TILES // RING + 2 * j + half + 1)
                        for p in range(PAIRS):
                            pool.wait_ge(z["combined"], first_tile + p + 1)
                            pool.sem_inc(z["gate"], 1)
                            for k in range(TOPK):
                                pool.indirect_dma_start(
                                    out=yg[:, p, k, :], out_offset=None, in_=y_dram[:, :],
                                    in_offset=bass.IndirectOffsetOnAxis(
                                        ap=cstage[:, half, p * TOPK + k:p * TOPK + k + 1], axis=0)
                                ).then_inc(z[f"g{p}"], 16)

            def attention():
                t = T

                def turn(i, u):
                    if there(i):
                        pool.wait_ge(t["rec"], i + 1)
                        pool.tensor_tensor(pr[:, u, :, :], pr[:, u, :, :],
                                           prec[:, u, :].unsqueeze(2).to_broadcast([P, NH, P]),
                                           ALU.mult).then_inc(t["norm"], 1)
                    b, q = i + PRE + 1, (u + PRE + 1) % 2
                    if there(b):
                        after(pool, t["combined"], b - 1)
                        pool.tensor_copy(cstage[:, q, 0:TOPK], slot_i[:, bass.ds(b, 1), :]
                                         .rearrange("p a k -> p (a k)")).then_inc(t["stage"], 1)
                        pool.wait_ge(t["stage"], b + 1)
                        pool.sem_inc(t["gate"], 1)
                        for k in range(TOPK):
                            pool.indirect_dma_start(
                                out=yg[:, q, k, :], out_offset=None, in_=y_dram[:, :],
                                in_offset=bass.IndirectOffsetOnAxis(ap=cstage[:, q, k:k + 1], axis=0)
                            ).then_inc(t[f"g{q}"], 16)
                    if u == 0:
                        after(pool, t["normed"], upto(i + 4))
                        after(pool, t["routed"], upto(i - 3))
                        pool.sem_inc(passed_pool, 1)
                        if there(i + 5) or there(i - POST + 1):
                            newton(pool, steps, var4[:, :], rstd4[:, :], nt4[:, :])
                            steps.did(pool.tensor_tensor(shift4[:, :], minus4[:, :], rstd4[:, :], ALU.mult))
                            steps.wait()
                        pool.sem_inc(t["rstd"], 2)
                    if u == 1:
                        pool.wait_ge(t["moments"], i - FIRST_TURN + 2)
                        pool.sem_inc(passed_pool, 1)
                        steps.did(pool.tensor_scalar(var4[:, :], mv4[:, :, 1], EPS, None, ALU.add))
                        steps.did(pool.tensor_scalar(minus4[:, :], mv4[:, :, 0], -1.0, None, ALU.mult))
                        steps.wait()
                        pool.sem_inc(t["taken"], 2)

                steps = Steps(pool, pool_steps, passed_pool)
                turns(pool, turn, steps, 3 + NEWTON)

            low_parts(0, E - 3)
            end_phase(pool, 0)
            low_parts(E - 3, E)
            numbers(0)
            end_phase(pool, 1)
            gather_rows(0)
            end_phase(pool, 2)
            attention()
            end_phase(pool, 3)
            numbers(1)
            end_phase(pool, 4)
            gather_rows(1)
            end_phase(pool, 5)
            gather_pairs(1, last)

        @block.scalar
        def _(a):
            def experts(r):
                a.sem_inc(r["rowsT_hi"], 2)
                a.sem_inc(r["hidT_hi"], 2)
                a.sem_inc(r["y_sb"], 2)

                def silu_s(p, s):
                    a.wait_ge(r["gu"], s + 1 + 2)
                    a.wait_ge(r["hid"], s + 1)
                    a.activation(gate[:, p, :], CC[:, 512 * p:512 * p + H], ACT.Silu).then_inc(r["silu"], 1)

                def rows_high(p, s):
                    a.wait_ge(r["rowsT"], s + 1 + RING)
                    a.wait_ge(r["gu"], s + 1)
                    a.activation(rowsT_hi[:, p, :], (A, B)[p][:, 0:D], ACT.Copy).then_inc(r["rowsT_hi"], 1)

                def hid_high(p, s):
                    a.wait_ge(r["hidT"], s + 1 + 2)
                    a.wait_ge(r["y"], s + 1)
                    a.activation(hidT_hi[:, p, :], (F, G)[p][0:HW, 0:2 * P], ACT.Copy).then_inc(r["hidT_hi"], 1)

                def y_s(u, s, round_):
                    a.wait_ge(r["y"], s + 1 + 2)
                    a.wait_ge(r[f"st{u % RING}"], 16 * (round_ + 1))
                    a.activation(y_sb[:, u % RING, :], SS[:, 512 * (u % 2):512 * (u % 2) + D], ACT.Copy
                                 ).then_inc(r["y_sb"], 1)

                a.preload_act_table(ACT.Silu)
                rows_high(0, 0)

                def step(u, s, j):
                    if is_tile(s + 1):
                        rows_high((u + 1) % 2, s + 1)
                    if is_tile(s):
                        silu_s(u % 2, s)
                    if is_tile(s - 1):
                        hid_high((u - 1) % 2, s - 1)
                    if is_tile(s - 2):
                        y_s(u - 2, s - 2, j + (u - 2) // RING)

                expert_steps(a, step)

            def attention():
                t = T

                def turn(i, u):
                    if there(i + 1):
                        b, q = i + 1, (u + 1) % 2
                        a.wait_ge(t["qh"], b + 1)
                        a.activation(qh, CC[:, 0:512], ACT.Copy, scale=SCALE).then_inc(t["qh_sb"], 1)
                        a.wait_ge(t["vh"], b + 1)
                        a.activation(vo[:, q, :], F[:, :], ACT.Copy).then_inc(t["vo"], 1)
                    if u == 1 and (there(i + 4) or there(i - POST) or there(i - POST + 1)):
                        a.wait_ge(t["rstd"], i - FIRST_TURN)
                        for b, dst, done, col in ((i + 3, ha, t["normed"], 0), (i - POST, hr, t["routed"], 2)):
                            for k in range(2):
                                if not there(b + k):
                                    continue
                                if col == 0:
                                    after(a, t["xT"], b + k - 1)
                                    place = k
                                else:
                                    after(a, t["hrT"], b + k - 1)
                                    place = 1 - k
                                    after(a, t[f"stored{place}"], 8 * (b - 1 if k == 0 else b + 1))
                                a.activation(dst[:, place, :], x_tile(b + k), ACT.Identity,
                                             bias=shift4[:, col + k:col + k + 1],
                                             scale=rstd4[:, col + k:col + k + 1]).then_inc(done, 1)
                    if there(i):
                        a.wait_ge(t["prT"], i + 1)
                        for half, done in enumerate(("prT_even", "prT_odd")):
                            a.activation(prT[:, 4 * half:4 * half + 4, :],
                                         CC[:, 512 * half:512 * (half + 1)].rearrange("p (h n) -> p h n", h=4),
                                         ACT.Copy).then_inc(t[done], 1)
                    if there(i + 3):
                        b, q = i + 3, (u + 3) % 2
                        a.wait_ge(t["xT"], b + 1)
                        if there(i - POST):
                            a.wait_ge(t["hrT"], i - POST + 1)
                        after(a, t["conv"], b - 1)
                        after(a, t["halo"], b - 1)
                        a.activation(xT[:, q, :, TAPS - 1:], A[:, 0:D].rearrange("p (c n) -> p c n", c=DC),
                                     ACT.Copy).then_inc(t["xT_sb"], 1)
                    if there(i - POST):
                        b = i - POST
                        a.wait_ge(t["hrT"], b + 1)
                        after(a, t["logits"], b)
                        a.activation(hT_sb[:, 0, :], A[:, D:2 * D], ACT.Copy).then_inc(t["hrT_sb"], 1)
                    if there(i + 1):
                        b, q = i + 1, (u + 1) % 2
                        a.wait_ge(t["max"], b + 1)
                        for h in range(NH):
                            e = a.activation(pr[:, q, h, :], pr[:, q, h, :], ACT.Exp,
                                             bias=nmax[:, q, h:h + 1], accum_out=psums[:, q, h:h + 1])
                        e.then_inc(t["exp"], 1)

                a.wait_ge(wprep, 1)
                a.activation(wvo_hi[:, :], A[0:W + 1, :], ACT.Copy).then_inc(wprep, 1)
                a.preload_act_table(ACT.Exp)
                turns(a, turn)

            def first_copies():
                def copy(p, t):
                    a.wait_ge(first["transposed"], t + 1)
                    a.activation(hT_sb[:, p, :], (A, B)[p][:, 0:D], ACT.Copy).then_inc(first["copied"], 1)

                a.preload_act_table(ACT.Copy)
                with a.Fori(0, TILES // 2 - E) as j:
                    for p in range(2):
                        copy(p, 2 * j + p)
                a.wait_ge(loaded, 16 * len(loads))
                with a.Fori(0, E) as e:
                    for p in range(2):
                        copy(p, TILES - 2 * E + 2 * e + p)
                    for whole, hi, _ in weight_parts(e):
                        a.activation(hi, whole, ACT.Copy).then_inc(high, 1)

            def difference(r):
                a.wait_ge(r["diff"], 1)
                a.activation(wtmp[:, 0, :], wtmp[:, 1, :], ACT.Exp).then_inc(r["expd"], 1)

            a.sem_inc(first["copied"], 2)
            first_copies()
            end_phase(a, 0)
            difference(R[0])
            end_phase(a, 1)
            experts(R[0])
            end_phase(a, 2)
            attention()
            end_phase(a, 3)
            difference(R[1])
            end_phase(a, 4)
            experts(R[1])
            end_phase(a, 5)

        @block.vector
        def _(v):
            st = Steps(v, dve)
            v.wait_ge(made, N_CONST)
            v.tensor_copy(iota_f[:, :], iota_i[:, :]).then_inc(const, 1)
            v.tensor_copy(part_f[:, :], part_i[:, :]).then_inc(const, 1)
            v.wait_ge(const, 2)
            v.tensor_scalar(erank[:, :], iota_f[:, 0:E], -float(E), None, ALU.add).then_inc(const, 1)
            v.tensor_scalar(number[:, :], iota_f[:, 0:TILES], float(P), part_f[:, 0:1], ALU.mult, ALU.add
                            ).then_inc(const, 1)
            v.wait_ge(const, 4)
            v.memset(at_i[:, :], 0)

            def first_norm():
                for g in range(GROUPS):
                    v.wait_ge(x_in[g], 16)
                    for u in range(GROUP):
                        st.did(v.bn_stats(stats[:, u, :], x_tile(GROUP * g + u)))
                    st.wait()
                    v.sem_inc(passed_dve, 1)
                    for u in range(GROUP):
                        st.did(v.bn_aggr(mv[:, u, :], stats[:, u, :]))
                    st.wait()
                    st.did(v.tensor_scalar(var[:, :], mv[:, :, 1], EPS, None, ALU.add))
                    st.wait()
                    newton(v, st, var[:, :], rstd[:, :], nt[:, :])
                    if g >= 2:
                        v.wait_ge(first[f"stored{g % 2}"], 16 * (g // 2))
                    for u in range(GROUP):
                        if g >= 2:
                            v.wait_ge(first["transposed"], GROUP * (g - 2) + u + 1)
                        v.tensor_scalar(h_rings[g % 2][:, u, :], x_tile(GROUP * g + u), mv[:, u, 0:1],
                                        rstd[:, u:u + 1], ALU.subtract, ALU.mult).then_inc(first["normed"], 1)

            def add_experts(z, t, q, rows_in):
                v.wait_ge(z[f"g{q}"], rows_in)
                for k in range(TOPK):
                    st.did(v.scalar_tensor_tensor(out=x_tile(t), in0=yg[:, q, k, :], scalar=wts[:, k, bass.ds(t, 1)],
                                                  in1=x_tile(t), op0=ALU.mult, op1=ALU.add))
                    st.wait()
                v.sem_inc(z["combined"], 1)

            def last_sum():
                v.sem_inc(last["combined"], PAIRS)
                with v.Fori(0, TILES // PAIRS) as j:
                    st.enter(j, PAIRS * TOPK)
                    for q in range(PAIRS):
                        add_experts(last, PAIRS * j + q, q, 16 * TOPK * (j + 1))
                        v.sem_inc(final, 1)
                st.leave(TILES // PAIRS)

            def route(L, from_psum):
                r = R[L]

                def step(i):
                    st.did(i)
                    st.wait()

                def over_e(ap):
                    return ap.unsqueeze(2).to_broadcast([P, TILES, E])

                if from_psum:
                    step(v.tensor_copy(lg[:, :, :], F[:, 0:TILES * E].rearrange("p (i e) -> p i e", e=E)))
                src = lg
                ranks = erank[:, :].unsqueeze(1).to_broadcast([P, TILES, E])
                for k in range(TOPK):
                    step(v.tensor_reduce(top[:, k, :], src[:, :, :], AX.X, ALU.max))
                    step(v.tensor_tensor(tmp[:, :, :], src[:, :, :], over_e(top[:, k, :]), ALU.is_equal))
                    step(v.tensor_tensor(tmp[:, :, :], tmp[:, :, :], ranks, ALU.mult))
                    step(v.tensor_reduce(pick[:, k, :], tmp[:, :, :], AX.X, ALU.min))
                    step(v.tensor_tensor(oh[:, k, :, :], over_e(pick[:, k, :]), ranks, ALU.is_equal))
                    if k == 0:
                        step(v.scalar_tensor_tensor(out=lg2[:, :, :], in0=oh[:, 0, :, :], scalar=-3.0e38,
                                                    in1=lg[:, :, :], op0=ALU.mult, op1=ALU.add))
                        src = lg2
                v.tensor_tensor(sel_bf[:, :].rearrange("p (i e) -> p i e", e=E), oh[:, 0, :, :], oh[:, 1, :, :],
                                ALU.add).then_inc(r["picked"], 1)
                v.tensor_tensor(wtmp[:, 1, :], top[:, 1, :], top[:, 0, :], ALU.subtract).then_inc(r["diff"], 1)
                v.wait_ge(r["counted"], 1)
                step(v.tensor_copy(tot[:, :, :], B[:, 0:TILES * E].rearrange("p (i e) -> p e i", e=E)))
                step(v.tensor_tensor_scan(cum[:, :, :].rearrange("p e i -> p (e i)"),
                                          tot[:, :, :].rearrange("p e i -> p (e i)"), zeros[:, :], 0.0,
                                          ALU.add, ALU.add))
                ends = cum[:, :, TILES - 1]
                step(v.tensor_copy(ecnt[:, 0:1], cum[:, 0, TILES - 1:TILES]))
                step(v.tensor_tensor(ecnt[:, 1:E], cum[:, 1:E, TILES - 1], cum[:, 0:E - 1, TILES - 1], ALU.subtract))
                step(v.tensor_scalar(etil[:, :], ecnt[:, :], P / 2 - 0.5, 1.0 / P, ALU.add, ALU.mult))
                step(v.tensor_scalar(etil[:, :], etil[:, :], MAGIC, MAGIC, ALU.add, ALU.subtract))
                step(v.tensor_tensor_scan(etcum[:, :], etil[:, :], zeros[:, 0:E], 0.0, ALU.add, ALU.add))
                step(v.tensor_tensor(eadj[:, :], etcum[:, :], etil[:, :], ALU.subtract))
                step(v.scalar_tensor_tensor(out=eadj[:, :], in0=eadj[:, :], scalar=float(P), in1=ecnt[:, :],
                                            op0=ALU.mult, op1=ALU.add))
                step(v.tensor_tensor(eadj[:, :], eadj[:, :], ends, ALU.subtract))
                step(v.tensor_tensor(cum[:, :, :], cum[:, :, :], tot[:, :, :], ALU.subtract))
                step(v.tensor_tensor(cum[:, :, :], cum[:, :, :], eadj[:, :].unsqueeze(2).to_broadcast([P, E, TILES]),
                                     ALU.add))
                step(v.tensor_tensor(lg[:, :, :], A[:, 0:TILES * E].rearrange("p (i e) -> p i e", e=E),
                                     cum[:, :, :].rearrange("p e i -> p i e"), ALU.add))
                for k in range(TOPK):
                    step(v.tensor_tensor(tmp[:, :, :], lg[:, :, :], oh[:, k, :, :], ALU.mult))
                    step(v.tensor_reduce(slot[:, k, :], tmp[:, :, :], AX.X, ALU.add))
                step(v.tensor_copy(slot_i[:, :, :].rearrange("p i k -> p k i"), slot[:, :, :]))
                step(v.tensor_scalar(stile[:, :, :], slot[:, :, :], 0.5 - P / 2, 1.0 / P, ALU.add, ALU.mult))
                step(v.tensor_scalar(stile[:, :, :], stile[:, :, :], MAGIC, MAGIC, ALU.add, ALU.subtract))
                step(v.scalar_tensor_tensor(out=slane[:, :, :], in0=stile[:, :, :], scalar=-float(P),
                                            in1=slot[:, :, :], op0=ALU.mult, op1=ALU.add))
                with v.Fori(0, TILES // BATCHED // 2) as j:
                    for p in range(2):
                        v.wait_ge(r["tabled"], 2 * j + p + 1)
                        at = bass.ds((2 * j + p) * BATCHED, BATCHED)
                        for where, onehot, width, done in ((stile, tile_oh, SLOT_TILES, "tiles"),
                                                           (slane, lane_oh, P, "lanes")):
                            for k in range(TOPK):
                                ins = v.tensor_tensor(
                                    onehot[:, p, k, :, :],
                                    iota_f[:, 0:width].unsqueeze(1).to_broadcast([P, BATCHED, width]),
                                    where[:, k, at].unsqueeze(2).to_broadcast([P, BATCHED, width]), ALU.is_equal)
                            ins.then_inc(r[done], 1)
                step(v.tensor_tensor(eidw[:, :, :], etcum[0:1, :].unsqueeze(1).to_broadcast([1, SLOT_TILES, E]),
                                     iota_f[0:1, 0:SLOT_TILES].unsqueeze(2).to_broadcast([1, SLOT_TILES, E]),
                                     ALU.is_le))
                step(v.tensor_reduce(eidf[:, :], eidw[:, :, 0:E - 1], AX.X, ALU.add))
                step(v.tensor_scalar(at_i[:, 0:SLOT_TILES], eidf[:, :], float(EW), None, ALU.mult))
                v.wait_ge(r["expd"], 1)
                step(v.tensor_scalar(wtmp[:, 1, :], wtmp[:, 0, :], 1.0, None, ALU.add))
                step(v.reciprocal(wtmp[:, 1, :], wtmp[:, 1, :]))
                step(v.tensor_scalar(wts[:, 0, :], wtmp[:, 1, :], 0.5, None, ALU.mult))
                step(v.tensor_tensor(wts[:, 1, :], wts[:, 0, :], wtmp[:, 0, :], ALU.mult))
                v.wait_ge(r["table"], 1)
                step(v.tensor_copy(tok_i[:, :], G[:, 0:SLOT_TILES]))

            def experts(r):
                v.sem_inc(r["hid"], 2)
                v.sem_inc(r["rowsT_lo"], 2)
                v.sem_inc(r["hidT_lo"], 2)

                def hid_s(p, s):
                    v.wait_ge(r["silu"], s + 1)
                    v.wait_ge(r["hidT"], s + 1)
                    v.tensor_tensor(hid[:, p, :], gate[:, p, :], CC[:, 512 * p + H:512 * p + GU], ALU.mult
                                    ).then_inc(r["hid"], 1)

                def rows_low(p, s):
                    v.wait_ge(r["rowsT_hi"], s + 1 + 2)
                    v.tensor_tensor(rowsT_lo[:, p, :], (A, B)[p][:, 0:D], rowsT_hi[:, p, :].bitcast(F32),
                                    ALU.subtract).then_inc(r["rowsT_lo"], 1)

                def hid_low(p, s):
                    v.wait_ge(r["hidT_hi"], s + 1 + 2)
                    v.tensor_tensor(hidT_lo[:, p, :], (F, G)[p][0:HW, 0:2 * P], hidT_hi[:, p, :].bitcast(F32),
                                    ALU.subtract).then_inc(r["hidT_lo"], 1)

                rows_low(0, 0)

                def step(u, s, j):
                    if is_tile(s + 1):
                        rows_low((u + 1) % 2, s + 1)
                    if is_tile(s):
                        hid_s(u % 2, s)
                    if is_tile(s - 1):
                        hid_low((u - 1) % 2, s - 1)

                expert_steps(v, step)

            def attention():
                t = T

                def stats_of(b, col):
                    st.did(v.bn_stats(stats[:, col, :], x_tile(b)))
                    st.wait()
                    v.sem_inc(passed_dve, 1)
                    st.did(v.bn_aggr(mv4[:, col, :], stats[:, col, :]))

                def turn(i, u):
                    if there(i + 1):
                        v.wait_ge(t["kh"], i + 2)
                        v.tensor_copy(kh, CC[:, 512:1024]).then_inc(t["kh_sb"], 1)
                    if there(i):
                        v.wait_ge(t["exp"], i + 1)
                        v.reciprocal(prec[:, u, :], psums[:, u, :]).then_inc(t["rec"], 1)
                    if there(i + 2):
                        v.wait_ge(t["conv"], i + 3)
                        v.tensor_scalar(qk[0:W, 0, :], B[0:W, 0:P], convb_sb[0:W, 0:1], None, ALU.add)
                        v.tensor_scalar(qk[0:W, 1, :], B[W:2 * W, 0:P], convb_sb[W:2 * W, 0:1], None, ALU.add)
                        st.did(v.tensor_scalar(vtap[:, :], B[W:2 * W, P + 1:2 * P + 1], convb_sb[W:2 * W, 1:2], None,
                                               ALU.add))
                        st.wait()
                        st.did(v.tensor_tensor(vT[:, :], B[0:W, P:2 * P], vtap[:, :], ALU.add))
                        st.wait()
                        st.did(v.tensor_copy(vT_hi[0:W, :], vT[:, :]))
                        st.wait()
                        v.tensor_tensor(vT_lo[0:W, :], vT[:, :], vT_hi[0:W, :].bitcast(F32), ALU.subtract
                                        ).then_inc(t["qkv"], 1)
                    if there(i + 1):
                        q = (u + 1) % 2
                        v.wait_ge(t["scores"], i + 2)
                        after(v, t["prT"], i)
                        st.did(v.tensor_tensor(pr[:, q, :, :], SS[:, :].rearrange("p (h s) -> p h s", s=P),
                                               mask[:, :].unsqueeze(1).to_broadcast([P, NH, P]), ALU.add))
                        st.wait()
                        st.did(v.tensor_reduce(nmax[:, q, :], pr[:, q, :, :], AX.X, ALU.max))
                        st.wait()
                        v.tensor_scalar(nmax[:, q, :], nmax[:, q, :], -1.0, None, ALU.mult).then_inc(t["max"], 1)
                    if there(i + 3):
                        b, q = i + 3, (u + 3) % 2
                        v.wait_ge(t["xT_sb"], b + 1)
                        after(v, t["conv"], b)
                        v.tensor_scalar(xT[:, 1 - q, :, 0:TAPS - 1], xT[:, q, :, P:P + TAPS - 1],
                                        keep[:, bass.ds(b, 1)], None, ALU.mult).then_inc(t["halo"], 1)
                    if there(i + PRE):
                        b, q = i + PRE, (u + PRE) % 2
                        add_experts(t, b, q, 8 * TOPK * (b - q + 2))
                        if u == 0:
                            after(v, t["taken"], i - FIRST_TURN + 1)
                            v.sem_inc(passed_dve, 1)
                        stats_of(b, u)
                    if there(i):
                        v.wait_ge(t["mha"], i + 1)
                        v.tensor_scalar(mhaT[0:W, :], F[0:W, 0:P], bo_sb[:, 0:1], None, ALU.add
                                        ).then_inc(t["mhaT"], 1)
                    if there(i - POST):
                        b = i - POST
                        v.wait_ge(t["logits"], b + 1)
                        v.tensor_copy(lg[:, bass.ds(b, 1), :].rearrange("p a e -> p (a e)"), B[:, LG_AT:LG_AT + E]
                                      ).then_inc(t["lg"], 1)
                    if there(i - 1):
                        b = i - 1
                        v.wait_ge(t["out"], b + 1)
                        st.did(v.tensor_tensor(x_tile(b), x_tile(b), G[:, 0:D], ALU.add))
                        st.wait()
                        v.sem_inc(t["res"], 1)
                        if u == 0:
                            after(v, t["taken"], i - FIRST_TURN + 1)
                            v.sem_inc(passed_dve, 1)
                        stats_of(b, 2 + u)
                    if u == 1:
                        st.wait()
                        v.sem_inc(t["moments"], 2)

                v.wait_ge(wprep, 2)
                v.tensor_tensor(wvo_lo[:, :], A[0:W + 1, :], wvo_hi[:, :].bitcast(F32), ALU.subtract).then_inc(wprep, 1)
                st.did(v.memset(mv4[:, :, :], 1.0))
                v.memset(xT[:, 0, :, 0:TAPS - 1], 0.0).then_inc(const, 1)
                turns(v, turn, st, 2 * (TOPK + 2 + 3 + 3 + 2))

            first_norm()
            end_phase(v, 0)
            v.wait_ge(loaded, 16 * len(loads))
            route(0, True)
            end_phase(v, 1)
            experts(R[0])
            end_phase(v, 2)
            attention()
            end_phase(v, 3)
            route(1, False)
            end_phase(v, 4)
            experts(R[1])
            end_phase(v, 5)
            last_sum()

        @block.tensor
        def _(pe):
            held_regs = [pe.alloc_register(f"weights_held{u}") for u in range(2)]
            next_regs = [pe.alloc_register(f"weights_next{u}") for u in range(RING)]

            def weights_vo():
                for h in range(NH):
                    i = pe.matmul(A[0:W + 1, h * W:(h + 1) * W], wvT_sb[:, h, :], wo_sb[:, h, :], start=True, stop=True)
                i.then_inc(wprep, 1)
                pe.wait_ge(wprep, 3)

            def first_router():
                z = first

                def turn(u, t):
                    pe.wait_ge(z["normed"], t + 1)
                    pe.wait_ge(z["copied"], t + 1)
                    for c in range(DC):
                        i = pe.transpose((A, B)[u % 2][:, c * P:(c + 1) * P],
                                         h_rings[u // GROUP][:, u % GROUP, c * P:(c + 1) * P], ident[:, :])
                    i.then_inc(z["transposed"], 1)

                def logits(p, t):
                    pe.wait_ge(z["copied"], t + 3)
                    for c in range(DC):
                        pe.matmul(F[:, bass.ds(t * E, E)], hT_sb[:, p, c * P:(c + 1) * P], rw_sb[:, c * E:(c + 1) * E],
                                  start=(c == 0), stop=(c == DC - 1))

                turn(0, 0)
                for u in range(1, 2 * GROUP):
                    turn(u, u)
                    logits(1 - u % 2, u - 1)
                with pe.Fori(1, GROUPS // 2) as g:
                    for u in range(2 * GROUP):
                        turn(u, 2 * GROUP * g + u)
                        logits(1 - u % 2, 2 * GROUP * g + u - 1)
                logits(1, TILES - 1)

            def route(L):
                r = R[L]
                pe.wait_ge(r["picked"], 1)
                pe.matmul(A[:, 0:TILES * E], before_bf[:, :], sel_bf[:, :], start=True, stop=True)
                pe.matmul(B[:, 0:TILES * E], ones_bf[:, :], sel_bf[:, :], start=True, stop=True).then_inc(r["counted"], 1)
                pe.matmul(G[:, 0:SLOT_TILES], zeros[:, 0:P], zeros[:, 0:SLOT_TILES], start=True, stop=False,
                          skip_group_check=True)
                pe.sem_inc(r["tabled"], 2)
                with pe.Fori(0, TILES // BATCHED // 2) as j:
                    for p in range(2):
                        pe.wait_ge(r["lanes"], 2 * j + p + 1)
                        pe.wait_ge(r["numbered"], 2 * j + p + 1)
                        for k in range(TOPK):
                            for n in range(BATCHED):
                                i = pe.matmul(G[:, 0:SLOT_TILES], lane_oh[:, p, k, n, :], tile_oh[:, p, k, n, :],
                                              start=False, stop=False, skip_group_check=True)
                        i.then_inc(r["tabled"], 1)
                pe.matmul(G[:, 0:SLOT_TILES], zeros[:, 0:P], zeros[:, 0:SLOT_TILES], start=False, stop=True,
                          skip_group_check=True).then_inc(r["table"], 1)

            def experts(r):
                pe.sem_inc(r["rowsT"], RING)
                pe.sem_inc(r["gu"], 2)
                pe.sem_inc(r["hidT"], 2)
                pe.sem_inc(r["y"], 2)

                def load_next(s):
                    pe.load(next_regs, at_i[0:1, bass.ds(s, RING)])

                def held(reg):
                    return pe.snap(reg, min_val=0, max_val=(E - 1) * EW)

                def turn_rows(u, s, grp):
                    pe.wait_ge(r[f"g{u % RING}"], 16 * (grp + 1))
                    pe.wait_ge(r["rowsT_lo"], s + 1)
                    for c in range(DC):
                        i = pe.transpose((A, B)[u % 2][:, c * P:(c + 1) * P], rows[:, u % RING, c * P:(c + 1) * P],
                                         ident[:, :])
                    i.then_inc(r["rowsT"], 1)

                def gate_up(u, s, e):
                    pe.wait_ge(r["rowsT_lo"], s + 1 + 2)
                    pe.wait_ge(r["hid"], s + 1)
                    n = 0
                    for c in range(DC):
                        at = bass.ds(e + c * GU, GU)
                        for rows_part, weights in ((rowsT_hi, w_hi[:, at]), (rowsT_hi, w_lo[:, at].bitcast(F32R)),
                                                   (rowsT_lo, w_hi[:, at])):
                            n += 1
                            i = pe.matmul(CC[:, 512 * (u % 2):512 * (u % 2) + GU],
                                          rows_part[:, u % 2, c * P:(c + 1) * P], weights,
                                          start=(n == 1), stop=(n == 3 * DC))
                    i.then_inc(r["gu"], 1)

                def turn_hid(u, s):
                    pe.wait_ge(r["hid"], s + 1 + 2)
                    pe.wait_ge(r["hidT_lo"], s + 1)
                    for c, (o, w) in enumerate(HC):
                        i = pe.transpose((F, G)[u % 2][0:w, c * P:(c + 1) * P], hid[:, u % 2, o:o + w], ident[:, :])
                    i.then_inc(r["hidT"], 1)

                def down(u, s, e):
                    pe.wait_ge(r["hidT_hi"], s + 1 + 2)
                    pe.wait_ge(r["y_sb"], s + 1)
                    acc = SS[:, 512 * (u % 2):512 * (u % 2) + D]
                    at = [bass.ds(e + DC * GU + c * D, D) for c in range(2)]
                    for c in range(2):
                        for part, weights in enumerate((w_hi[0:HW, at[c]], w_lo[0:HW, at[c]].bitcast(F32R))):
                            pe.matmul(acc, hidT_hi[:, u % 2, c * P:(c + 1) * P], weights,
                                      start=(c == 0 and part == 0), stop=False)
                    pe.wait_ge(r["hidT_lo"], s + 1 + 2)
                    for c in range(2):
                        i = pe.matmul(acc, hidT_lo[:, u % 2, c * P:(c + 1) * P], w_hi[0:HW, at[c]], start=False,
                                      stop=(c == 1))
                    i.then_inc(r["y"], 1)

                def step(u, s, j, at_s, at_done):
                    if is_tile(s + 1):
                        turn_rows(u + 1, s + 1, j + (u + 1) // RING)
                    if is_tile(s):
                        gate_up(u, s, at_s)
                    if is_tile(s - 1):
                        turn_hid(u - 1, s - 1)
                    if is_tile(s - 2):
                        down(u - 2, s - 2, at_done)

                turn_rows(0, 0, 0)
                pe.load(held_regs, at_i[0:1, 0:2])
                load_next(2)
                at = [held(reg) for reg in held_regs]
                for s in range(2):
                    step(s, s, 0, at[s], None)
                with pe.Fori(0, ROUNDS) as j:
                    at = [held(reg) for reg in held_regs + next_regs]
                    for u in range(2, 2 + RING):
                        if u == 1 + RING:
                            load_next(RING * (j + 1) + 2)
                        step(u, RING * j + u, j, at[u], at[u - 2])
                    for k in range(2):
                        pe.reg_mov(held_regs[k], at[RING + k])
                at = [held(reg) for reg in held_regs + next_regs]
                for u in range(2, 2 + RING):
                    s = RING * ROUNDS + u
                    step(s, s, 0, at[u], at[u - 2])

            def attention():
                t = T

                def turn(i, u):
                    if there(i + 1):
                        b, q = i + 1, (u + 1) % 2
                        pe.wait_ge(t["qkv"], b + 1)
                        after(pe, t["prT_odd"], i)
                        for n, done in enumerate(("qh", "kh")):
                            for m in range(4):
                                x = pe.matmul(CC[:, 512 * n + m * P:512 * n + (m + 1) * P],
                                              wqk_sb[:, n, m * P:(m + 1) * P], qk[:, n, :], start=True, stop=True)
                            x.then_inc(t[done], 1)
                        after(pe, t["mhaT"], i)
                        after(pe, t["vo"], b)
                        for n, (part, weights) in enumerate(((vT_hi, wvo_hi), (vT_hi, wvo_lo), (vT_lo, wvo_hi))):
                            x = pe.matmul(F[:, :], part[:, :], weights[:, :], start=(n == 0), stop=(n == 2))
                        x.then_inc(t["vh"], 1)
                    if there(i + 2):
                        b, q = i + 2, u
                        pe.wait_ge(t["xT_sb"], b + 1)
                        after(pe, t["halo"], b)
                        after(pe, t["qkv"], b)
                        after(pe, t["lg"], i - POST)
                        for c in range(DC):
                            for k in range(TAPS):
                                pe.matmul(B[:, 0:P], conv_sb[:, c, k * P:(k + 1) * P], xT[:, q, c, k:k + P],
                                          start=(c == 0 and k == 0), stop=(c == DC - 1 and k == TAPS - 1))
                        for c in range(DC):
                            pe.matmul(B[:, P:2 * P + 1], conv_sb[:, c, V_AT:V_AT + P], xT[:, q, c, 0:P + 1],
                                      start=(c == 0), stop=False, skip_group_check=True)
                        for c in range(DC):
                            x = pe.matmul(B[0:W, P:2 * P], conv_sb[:, c, V_AT + P:], xT[:, q, c, TAPS - 1:],
                                          start=False, stop=(c == DC - 1), skip_group_check=True)
                        x.then_inc(t["conv"], 1)
                    if there(i + 1):
                        b = i + 1
                        pe.wait_ge(t["qh_sb"], b + 1)
                        pe.wait_ge(t["kh_sb"], b + 1)
                        after(pe, t["max"], b)
                        for h in range(NH):
                            lo, at, m = KD * (h % 2), HEAD_AT[h], h // 2
                            x = pe.matmul(SS[:, at * P:(at + 1) * P], qh[lo:lo + KD, m * P:(m + 1) * P],
                                          kh[lo:lo + KD, m * P:(m + 1) * P], start=True, stop=True)
                        x.then_inc(t["scores"], 1)
                    if there(i):
                        pe.wait_ge(t["norm"], i + 1)
                        for h in range(NH):
                            x = pe.transpose(CC[:, h * P:(h + 1) * P], pr[:, u, h, :], ident[:, :])
                        x.then_inc(t["prT"], 1)
                    if there(i + 3):
                        b, q = i + 3, (u + 1) % 2
                        pe.wait_ge(t["normed"], b + 1)
                        after(pe, t["xT_sb"], b)
                        after(pe, t["hrT_sb"], i - POST)
                        for c in range(DC):
                            x = pe.transpose(A[:, c * P:(c + 1) * P], ha[:, q, c * P:(c + 1) * P], ident[:, :])
                        x.then_inc(t["xT"], 1)
                    if there(i - POST):
                        b, q = i - POST, (u + POST) % 2
                        pe.wait_ge(t["routed"], b + 1)
                        after(pe, t["hrT_sb"], b)
                        if not there(i + 3):
                            pe.wait_ge(t["xT_sb"], TILES)
                        for c in range(DC):
                            x = pe.transpose(A[:, D + c * P:D + (c + 1) * P], hr[:, u, c * P:(c + 1) * P],
                                             ident[:, :])
                        x.then_inc(t["hrT"], 1)
                    if there(i - 1):
                        after(pe, t["res"], i - 1)
                        pe.wait_ge(t["mhaT"], i)
                        pe.matmul(G[:, 0:D], mhaT[:, :], proj_sb[:, :], start=True, stop=True
                                  ).then_inc(t["out"], 1)
                    if there(i):
                        pe.wait_ge(t["vo"], i + 2 if there(i + 1) else i + 1)
                        for n, h in enumerate(list(range(0, NH, 2)) + list(range(1, NH, 2))):
                            pe.wait_ge(t["prT_even" if n < 4 else "prT_odd"], i + 1)
                            x = pe.matmul(F[0:W, 0:P], vo[:, u, h * W:(h + 1) * W], prT[:, HEAD_AT[h], :],
                                          start=(n == 0), stop=(n == NH - 1))
                        x.then_inc(t["mha"], 1)
                    if there(i - POST):
                        pe.wait_ge(t["hrT_sb"], i - POST + 1)
                        if there(i + 2):
                            pe.wait_ge(t["qkv"], i + 3)
                        else:
                            after(pe, t["lg"], i - POST)
                        for c in range(DC):
                            x = pe.matmul(B[:, LG_AT:LG_AT + E], hT_sb[:, 0, c * P:(c + 1) * P],
                                          rw_sb[:, c * E:(c + 1) * E], start=(c == 0), stop=(c == DC - 1))
                        x.then_inc(t["logits"], 1)

                turns(pe, turn)

            pe.wait_ge(rw_in, 16)
            pe.wait_ge(const, 4)
            first_router()
            pe.wait_ge(loaded, 16 * len(loads))
            end_phase(pe, 0)
            route(0)
            pe.wait_ge(low, 2 * E)
            end_phase(pe, 1)
            experts(R[0])
            end_phase(pe, 2)
            weights_vo()
            pe.wait_ge(const, 5)
            attention()
            end_phase(pe, 3)
            route(1)
            end_phase(pe, 4)
            experts(R[1])
            end_phase(pe, 5)


def kernel(**inputs):
    import numpy as _np
    import concourse.bacc as _bacc
    from concourse import mybir as _mybir
    from concourse.bass_utils import run_bass_kernel_spmd as _run

    a = {n: _np.asarray(v) for n, v in inputs.items()}
    f32 = {
        "x": a["L0_attn_x"],
        "conv_w": _np.concatenate([part.reshape(TAPS, DC, P, -1).transpose(2, 1, 0, 3).reshape(P, DC, -1) for part in
                                   (a["L0_attn_conv_w"][:, :, 0:2 * W], a["L0_attn_conv_w"][:, :, 2 * W:])], 2),
        "conv_b": a["L0_attn_conv_b"].reshape(3 * W, 1),
        "wq": a["L0_attn_wq"].reshape(W, NH * KD),
        "wk": a["L0_attn_wk"].reshape(W, NH * KD),
        "wvT": _np.concatenate([a["L0_attn_wv"].transpose(2, 1, 0), a["L0_attn_bv"].T.reshape(KD, NH, 1)], 2),
        "wo": a["L0_attn_wo"].transpose(1, 0, 2),
        "bq": a["L0_attn_bq"].reshape(1, NH * KD),
        "bk": a["L0_attn_bk"].reshape(1, NH * KD),
        "bo": a["L0_attn_bo"].reshape(W, 1),
        "proj_w": a["L0_attn_proj_w"],
        "proj_b": a["L0_attn_proj_b"].reshape(1, D),
        "gupT": a["L0_ffn_gate_up_proj"].reshape(E, GU, DC, P).transpose(3, 0, 2, 1).reshape(P, E, DC * GU),
        "dpT": a["L0_ffn_down_proj"].transpose(2, 0, 1),
        "rwT": a["L0_ffn_router_w"].reshape(E, DC, P).transpose(2, 1, 0).reshape(P, DC * E),
    }
    nc = _bacc.Bacc("TRN2", target_bir_lowering=False, num_devices=1)
    arrays, args = {}, []
    for name, v in f32.items():
        v = _np.ascontiguousarray(v)
        arrays[f"in_{name}_dram"] = v
        args.append(nc.dram_tensor(f"in_{name}_dram", v.shape, _mybir.dt.from_np(v.dtype), kind="ExternalInput").ap())
    args.append(nc.dram_tensor("out_0_dram", (BATCH, SEQ, D), F32, kind="ExternalOutput").ap())
    args.append(nc.dram_tensor("h_rows", (TOKENS, D), F32, kind="Internal").ap())
    args.append(nc.dram_tensor("y_rows", (SLOT_TILES * P, D), F32, kind="Internal").ap())
    macaron_kernel(nc, *args)
    r = _run(nc, [arrays], core_ids=[0])
    return r.results[0]["out_0_dram"]
```
